# Optimizing a Trainium2 kernel written in Bass

```python
import numpy as np
import jax
import jax.numpy as jnp

def _softmax(x, axis=-1):
    return jax.nn.softmax(x, axis=axis)

def _gelu(x):
    return jax.nn.gelu(x, approximate=True)

def _silu(x):
    return jax.nn.silu(x)

def _sigmoid(x):
    return jax.nn.sigmoid(x)

def _layernorm(x, axis=-1, eps=1e-05):
    m = jnp.mean(x, axis=axis, keepdims=True)
    v = jnp.var(x, axis=axis, keepdims=True)
    return (x - m) / jnp.sqrt(v + eps)

def _scatter_add(tgt, idx, src, axis=0):
    return tgt.at[idx].add(src)

def _segment_sum(src, seg, n):
    return jax.ops.segment_sum(src, seg, n)
kernel_name = 'mk_early_fusion_d1_tok_img768_r4_0cab35'

def setup_inputs(seed: int=0):
    np.random.seed(seed)
    _w = jnp.asarray

    def _rec_inputs():
        import jax
        import jax.numpy as jnp
        _rk = jax.random.key(seed)
        x = -1.80045e-05 + 0.999906 * jax.random.normal(jax.random.fold_in(_rk, 1), (4, 3, 96, 96), jnp.float32)
        txt = 0.261128 + 1.19657 * jax.random.normal(jax.random.fold_in(_rk, 2), (4, 512, 192), jnp.float32)
        return (x, txt)
    x, txt = _rec_inputs()

    def _L0_tok_setup():
        import jax, jax.numpy as jnp
        import numpy as np
        IMAGE_SIZE = 96
        PATCH = 16
        CHANNELS = 3
        TOKEN_DIM = 192
        NUM_PATCHES = (IMAGE_SIZE // PATCH) ** 2
        PATCH_DIM = CHANNELS * PATCH * PATCH
        N_TOKENS = NUM_PATCHES + 1

        def _fixed_pos_embedding(n_tokens, dim):
            i = np.arange(n_tokens, dtype=np.float32)[:, None]
            j = np.arange(dim, dtype=np.float32)[None, :]
            j_even = np.where(j % 2 == 0, j, j - 1)
            angle = i / np.power(10000.0, j_even / dim)
            tab = np.where(j % 2 == 0, np.sin(angle), np.cos(angle)).astype(np.float32)
            return jnp.asarray(tab)

        def _make_patches(image):
            B, C, H, Wd = image.shape
            p = PATCH
            hp, wp = (H // p, Wd // p)
            x = image.reshape(B, C, hp, p, wp, p)
            x = x.transpose(0, 1, 2, 4, 3, 5)
            return x.reshape(B, hp * wp, C * p * p)
        key = jax.random.key(seed)
        k_img, k_w, k_b, k_cls = jax.random.split(key, 4)
        image = jax.random.normal(k_img, (128, CHANNELS, IMAGE_SIZE, IMAGE_SIZE), dtype=jnp.float32)
        W = jax.random.normal(k_w, (TOKEN_DIM, PATCH_DIM), dtype=jnp.float32) / np.sqrt(PATCH_DIM)
        b = jax.random.normal(k_b, (TOKEN_DIM,), dtype=jnp.float32) * 0.01
        class_token = jax.random.normal(k_cls, (1, TOKEN_DIM), dtype=jnp.float32)
        pos_embedding = _fixed_pos_embedding(N_TOKENS, TOKEN_DIM)
        return {'image': image, 'W': W, 'b': b, 'class_token': class_token, 'pos_embedding': pos_embedding}
    _L0_tok_all = _L0_tok_setup()
    _L0_tok_in = {k: v for k, v in _L0_tok_all.items() if k in ('W', 'b', 'class_token', 'pos_embedding')}
    del _L0_tok_all

    def _L0_attn_setup():
        import jax, jax.numpy as jnp
        import numpy as np
        EMBED_DIM = 192
        NUM_HEADS = 12
        HEAD_DIM = EMBED_DIM // NUM_HEADS
        MEMORY_SIZE = 64
        B, T = (8, 256)
        key = jax.random.key(seed)
        ks = jax.random.split(key, 8)
        s = 0.02
        return {'x': jax.random.normal(ks[0], (B, T, EMBED_DIM), dtype=jnp.float32), 'w_qkv': jax.random.normal(ks[1], (EMBED_DIM, 3 * EMBED_DIM), dtype=jnp.float32) * s, 'b_qkv': jax.random.normal(ks[2], (3 * EMBED_DIM,), dtype=jnp.float32) * s, 'w_out': jax.random.normal(ks[3], (EMBED_DIM, EMBED_DIM), dtype=jnp.float32) * s, 'b_out': jax.random.normal(ks[4], (EMBED_DIM,), dtype=jnp.float32) * s, 'w_mem': jax.random.normal(ks[5], (EMBED_DIM, EMBED_DIM), dtype=jnp.float32) * s, 'b_mem': jax.random.normal(ks[6], (EMBED_DIM,), dtype=jnp.float32) * s, 'memory': jax.random.normal(ks[7], (1, MEMORY_SIZE, EMBED_DIM), dtype=jnp.float32)}
    _L0_attn_all = _L0_attn_setup()
    _L0_attn_in = {k: v for k, v in _L0_attn_all.items() if k in ('w_qkv', 'b_qkv', 'w_out', 'b_out', 'w_mem', 'b_mem', 'memory')}
    del _L0_attn_all

    def _L0_ffn_setup():
        import jax, jax.numpy as jnp
        import numpy as np
        NUM_EXPERTS = 8
        TOP_K = 2
        CAP_FACTOR = 1.0
        D_MODEL = 192
        D_FF = 768
        key = jax.random.key(seed)
        k0, k1, k2, k3 = jax.random.split(key, 4)
        B, S, D = (1, 512, D_MODEL)
        inputs = jax.random.normal(k0, (B, S, D), dtype=jnp.float32)
        router_w = jax.random.normal(k1, (NUM_EXPERTS, D), dtype=jnp.float32) * D ** (-0.5)
        w1 = jax.random.normal(k2, (NUM_EXPERTS, D, D_FF), dtype=jnp.float32) * D ** (-0.5)
        w2 = jax.random.normal(k3, (NUM_EXPERTS, D_FF, D), dtype=jnp.float32) * D_FF ** (-0.5)
        return {'inputs': inputs, 'router_w': router_w, 'w1': w1, 'w2': w2}
    _L0_ffn_all = _L0_ffn_setup()
    _L0_ffn_in = {k: v for k, v in _L0_ffn_all.items() if k in ('router_w', 'w1', 'w2')}
    del _L0_ffn_all
    return {'x': x, 'txt': txt, 'L0_tok_W': _L0_tok_in['W'], 'L0_tok_b': _L0_tok_in['b'], 'L0_tok_class_token': _L0_tok_in['class_token'], 'L0_tok_pos_embedding': _L0_tok_in['pos_embedding'], 'L0_attn_w_qkv': _L0_attn_in['w_qkv'], 'L0_attn_b_qkv': _L0_attn_in['b_qkv'], 'L0_attn_w_out': _L0_attn_in['w_out'], 'L0_attn_b_out': _L0_attn_in['b_out'], 'L0_attn_w_mem': _L0_attn_in['w_mem'], 'L0_attn_b_mem': _L0_attn_in['b_mem'], 'L0_attn_memory': _L0_attn_in['memory'], 'L0_ffn_router_w': _L0_ffn_in['router_w'], 'L0_ffn_w1': _L0_ffn_in['w1'], 'L0_ffn_w2': _L0_ffn_in['w2']}

def reference(x, txt, L0_tok_W, L0_tok_b, L0_tok_class_token, L0_tok_pos_embedding, L0_attn_w_qkv, L0_attn_b_qkv, L0_attn_w_out, L0_attn_b_out, L0_attn_w_mem, L0_attn_b_mem, L0_attn_memory, L0_ffn_router_w, L0_ffn_w1, L0_ffn_w2):
    import jax
    import jax.numpy as jnp

    def _L0_tok_ref(image, W, b, class_token, pos_embedding):
        import jax, jax.numpy as jnp
        import numpy as np
        IMAGE_SIZE = 96
        PATCH = 16
        CHANNELS = 3
        TOKEN_DIM = 192
        NUM_PATCHES = (IMAGE_SIZE // PATCH) ** 2
        PATCH_DIM = CHANNELS * PATCH * PATCH
        N_TOKENS = NUM_PATCHES + 1

        def _fixed_pos_embedding(n_tokens, dim):
            i = np.arange(n_tokens, dtype=np.float32)[:, None]
            j = np.arange(dim, dtype=np.float32)[None, :]
            j_even = np.where(j % 2 == 0, j, j - 1)
            angle = i / np.power(10000.0, j_even / dim)
            tab = np.where(j % 2 == 0, np.sin(angle), np.cos(angle)).astype(np.float32)
            return jnp.asarray(tab)

        def _make_patches(image):
            B, C, H, Wd = image.shape
            p = PATCH
            hp, wp = (H // p, Wd // p)
            x = image.reshape(B, C, hp, p, wp, p)
            x = x.transpose(0, 1, 2, 4, 3, 5)
            return x.reshape(B, hp * wp, C * p * p)
        patches = _make_patches(image)
        tokens = jnp.einsum('bnd,td->bnt', patches, W) + b
        B = tokens.shape[0]
        cls = jnp.broadcast_to(class_token[None, :, :], (B, 1, TOKEN_DIM))
        tokens = jnp.concatenate([cls, tokens], axis=1)
        return tokens + pos_embedding[None, :, :]

    def _L0_attn_ref(x, w_qkv, b_qkv, w_out, b_out, w_mem, b_mem, memory):
        import jax, jax.numpy as jnp
        import numpy as np
        EMBED_DIM = 192
        NUM_HEADS = 12
        HEAD_DIM = EMBED_DIM // NUM_HEADS
        MEMORY_SIZE = 64
        B, T = (8, 256)
        Bx, Tx, C = x.shape
        H, D = (NUM_HEADS, HEAD_DIM)
        scale = 1.0 / np.sqrt(D).astype(np.float32)
        qkv = (x @ w_qkv + b_qkv).reshape(Bx, Tx, 3, H, D)
        qkv = jnp.transpose(qkv, (2, 0, 3, 1, 4))
        q, k, v = (qkv[0], qkv[1], qkv[2])
        scores = jnp.einsum('bhqd,bhkd->bhqk', q, k) * scale
        local_out = jnp.einsum('bhqk,bhkd->bhqd', jax.nn.softmax(scores, axis=-1), v)
        mem = memory @ w_mem + b_mem
        mem = jnp.broadcast_to(mem, (Bx, MEMORY_SIZE, C))
        mem_kv = jnp.transpose(mem.reshape(Bx, MEMORY_SIZE, H, D), (0, 2, 1, 3))
        mem_scores = jnp.einsum('bhqd,bhmd->bhqm', q, mem_kv) * scale
        mem_out = jnp.einsum('bhqm,bhmd->bhqd', jax.nn.softmax(mem_scores, axis=-1), mem_kv)
        out = (local_out + mem_out).transpose(0, 2, 1, 3).reshape(Bx, Tx, C)
        return out @ w_out + b_out

    def _L0_ffn_ref(inputs, router_w, w1, w2):
        import jax, jax.numpy as jnp
        import numpy as np
        NUM_EXPERTS = 8
        TOP_K = 2
        CAP_FACTOR = 1.0
        D_MODEL = 192
        D_FF = 768
        B, S, D = inputs.shape
        x = inputs.reshape(-1, D)
        N = x.shape[0]
        logits = x @ router_w.T
        probs = jax.nn.softmax(logits.astype(jnp.float32), axis=-1)
        weights, sel = jax.lax.top_k(probs, TOP_K)
        cap = int(CAP_FACTOR * N * TOP_K) + 1
        n_real = N * TOP_K
        expert_flat = sel.reshape(-1)
        weight_flat = weights.reshape(-1)
        token_idx = jnp.repeat(jnp.arange(N), TOP_K)
        pad = cap - n_real
        expert_flat = jnp.pad(expert_flat, (0, pad))
        weight_flat = jnp.pad(weight_flat, (0, pad))
        token_idx = jnp.pad(token_idx, (0, pad))
        valid = jnp.arange(cap) < n_real
        toks = x[token_idx]

        def mlp(w1e, w2e):
            return jax.nn.gelu(toks @ w1e) @ w2e
        ys = jax.vmap(mlp)(w1, w2)
        gate = (weight_flat * valid.astype(weight_flat.dtype)).astype(toks.dtype)
        res = ys[expert_flat, jnp.arange(cap)] * gate[:, None]
        out = jnp.zeros((N, D), dtype=inputs.dtype).at[token_idx].add(res)
        return out.reshape(B, S, D)
    h = _L0_tok_ref(x, L0_tok_W, L0_tok_b, L0_tok_class_token, L0_tok_pos_embedding)
    h = jnp.concatenate([h, txt], axis=1)
    h = h + _L0_attn_ref(_layernorm(h, axis=-1), L0_attn_w_qkv, L0_attn_b_qkv, L0_attn_w_out, L0_attn_b_out, L0_attn_w_mem, L0_attn_b_mem, L0_attn_memory)
    h = h + _L0_ffn_ref(_layernorm(h, axis=-1), L0_ffn_router_w, L0_ffn_w1, L0_ffn_w2)
    return h

_drawn_inputs = setup_inputs


def setup_inputs(seed=0):
    import zlib

    import numpy as np

    out = dict(_drawn_inputs(seed))
    spreads = {}
    factors = {'L0_tok_b': 8.0,
     'L0_attn_w_qkv': 7.942,
     'L0_attn_b_qkv': 4.686,
     'L0_attn_w_out': 3.642,
     'L0_attn_w_mem': 4.716,
     'L0_attn_b_mem': 19.793,
     'L0_attn_memory': 5.135,
     'L0_attn_b_out': 21.978}
    for name, (base, spread) in spreads.items():
        noise = np.random.default_rng([zlib.crc32(name.encode()), seed]).standard_normal(out[name].shape)
        drawn = base * np.exp(spread * noise) if base else spread * noise
        out[name] = jnp.asarray(drawn.astype(out[name].dtype))
    for name, factor in factors.items():
        out[name] = (out[name] * factor).astype(out[name].dtype)
    return out
```

```python
from contextlib import ExitStack

import concourse.bass as bass
from concourse import mybir
from concourse.alu_op_type import AluOpType as ALU

F32 = mybir.dt.float32
BF16 = mybir.dt.bfloat16
U32 = mybir.dt.uint32
I32 = mybir.dt.int32
ACT = mybir.ActivationFunctionType
AX = mybir.AxisListType.X

P = 128
B = 4
D = 192
DL = D - P
H, HD = 12, 16
NPATCH = 36
NIMG = NPATCH + 1
NTXT = 512
T = NIMG + NTXT
TT = 5
NT = B * TT
PD = 768
PC = PD // P
MEM = 64
GH = 4
G = H // GH
KQ = 6 * HD
KM = KQ + 4
KEYS = 5 * P
QC = 183
NC = T // QC
VW = 32
NE, DFF, TOPK = 8, 768, 2
FC = DFF // P
SLOT_TILES = (B * T * TOPK + NE * (P - 1)) // P
SLOTS = SLOT_TILES * P
EXP_TILES = (B * T + P - 1) // P
EPS = 1e-5
ZN = 14
R = 3

C_ID, C_TRI, C_ONE = 0, P, 2 * P
C_PREF = 3 * P
C_TAU = C_PREF + NE
C_K = C_TAU + SLOT_TILES
C_VALID = C_K + EXP_TILES
C_SEL = C_VALID + NT
C_N = C_SEL + NIMG


def rows_of(t):
    return P if t < TT - 1 else NIMG


def plan():
    front = lambda b: [s for t in range(TT + 2) for s in (
        ([("xT", b * TT + t)] if t < TT else []) +
        ([("qkv", b * TT + t), ("split", b * TT + t)] if t < TT else []) +
        ([("stack", b * TT + t - 1)] if 1 <= t <= TT else []))]
    maxima = lambda g: [("max", g, t, j) for t in range(TT) for j in range(GH + 1)] + [("negmax", g)]
    merge = lambda b: [s for t in range(TT + 2) for s in (
        ([("norm", b * TT + t)] if t < TT else []) +
        ([("attT", b * TT + t - 1)] if 1 <= t <= TT else []) +
        ([("proj", b * TT + t - 2)] if 2 <= t else []))]
    gate = lambda b: [("rstd", b)] + [s for t in range(TT + 2) for s in (
        ([("ln2", b * TT + t)] if t < TT else []) +
        ([("ln2T", b * TT + t - 1)] if 1 <= t <= TT else []) +
        ([("router", b * TT + t - 2)] if 2 <= t else []))]
    order = front(0) + maxima(0) + [("maxT", 0)] + maxima(1)
    units = TT * NC
    NG = B * G
    for g in range(NG):
        b = g // G
        fill = []
        if g + 1 < NG:
            fill.append(("maxT", g + 1))
        later = maxima(g + 2) if g + 2 < NG else []
        other = []
        if g % G == 0 and b + 1 < B:
            other = front(b + 1)
        if g % G == 1 and b > 0:
            other = merge(b - 1)
        if g % G == 2 and b > 0:
            other = gate(b - 1)
        n1, n2 = len(later), len(other)
        both = sorted([((i + 0.5) / n1, 0, s) for i, s in enumerate(later)] +
                      [((i + 0.5) / n2, 1, s) for i, s in enumerate(other)], key=lambda x: x[:2])
        fill += [s for _, _, s in both]
        order.append(("score", g * units))
        done = 0
        for u in range(units):
            n = g * units + u
            if u + 1 < units:
                order.append(("score", n + 1))
            upto = (u + 1) * len(fill) // units
            order += fill[done:upto]
            done = upto
            order.append(("value", n))
            if u % TT == TT - 1:
                order.append(("keep", n // TT))
    order += merge(B - 1) + gate(B - 1)
    return order


ORDER = plan()
JOBS = {"img": "DD", "mem": "AA", "memT": "AA", "xT": "A", "qkv": "AA", "stack": "AADD", "max": "D",
        "maxT": "A", "norm": "DD", "attT": "A", "proj": "D", "ln2T": "A", "router": "D", "rank": "DD"}


def ring_plan():
    place, drains, count = {}, [], {"A": 0, "D": 0}
    for s in [("img",), ("mem",), ("memT",)] + ORDER + [("rank",)]:
        for part, who in enumerate(JOBS.get(s[0], "")):
            count[who] += 1
            place[s + (part,)] = len(drains)
            drains.append((who, count[who]))
    return place, drains


PLACE, DRAINS = ring_plan()


def build(nc, a, out):
    ctx = ExitStack()
    sb = lambda name, shape, dt=F32: ctx.enter_context(nc.sbuf_tensor(name, shape, dt))
    sem = lambda name: ctx.enter_context(nc.semaphore(name))
    with ctx:
        cst = sb("cst", [P, C_N])
        ident, tri, ones = cst[:, C_ID:C_ID + P], cst[:, C_TRI:C_TRI + P], cst[:, C_ONE:C_ONE + P]
        identb = sb("identb", [P, P], BF16)
        h_all = sb("h_all", [P, NT, D])
        xn = sb("xn", [P, NT, D])
        patchT = sb("patchT", [P, PC, B, NIMG])
        tokw = sb("tokw", [P, PC, D])
        clsb = sb("clsb", [2, D])
        pos = sb("pos", [NIMG, D])
        wqkv = [sb("wqkv_a", [P, 3 * D]), sb("wqkv_b", [DL + 1, 3 * D])]
        wout = [sb("wout_a", [P, D]), sb("wout_b", [DL + 1, D])]
        wmem = [sb("wmem_a", [P, D]), sb("wmem_b", [DL + 1, D])]
        memT = [sb("memT_a", [P, MEM]), sb("memT_b", [DL + 1, MEM])]
        wr = [sb("wr_a", [P, NE]), sb("wr_b", [DL, NE])]
        stats = sb("stats", [P, NT, 6])
        mv = sb("mv", [P, NT, 2])
        ve = sb("ve", [P, NT])
        lnv = sb("lnv", [P, NT])
        r0 = sb("r0", [P, NT])
        rn = sb("rn", [P, NT])
        rstd = sb("rstd", [P, NT])
        xT = [sb("xT_a", [P, 2, P]), sb("xT_b", [DL + 1, 2, P])]
        qk = sb("qk", [P, 2, 2 * D])
        hi = sb("hi", [P, 2 * D], BF16)
        mid = sb("mid", [P, 2 * D], BF16)
        rest = sb("rest", [P, 2 * D])
        qs = sb("qs", [P, 2, H, KQ], BF16)
        ks = sb("ks", [P, 2, H, KM], BF16)
        mx = sb("mx", [P, 2, TT, GH])
        mt = sb("mt", [P, 2, TT, GH, 2])
        mp = sb("mp", [P, 2, TT, GH, 4], BF16)
        mrow = sb("mrow", [4 * GH, T], BF16)
        pr = sb("pr", [P, 3, 2, 2 * QC])
        rec = sb("rec", [P, 2, G, GH])
        prod = sb("prod", [P, 2, G, GH, HD])
        att = sb("att", [P, 2, D])
        logit = sb("logit", [P, NT, NE])

        n_q, n_k, n_v, n_o = H * T, H * KEYS // 2 * 2, 6 * H * VW, G * 2 * T
        region = sb("region", [P, n_q + n_k + 2 * n_v + 2 * n_o])
        o = 0
        qst = region[:, 0:n_q].bitcast(BF16).rearrange("p (s h t) -> p s h t", s=2, h=H)
        o += n_q
        kst = region[:, o:o + n_k].bitcast(BF16).rearrange("p (s h t) -> p s h t", s=2, h=H)
        o += n_k
        val = region[:, o:o + 2 * n_v].rearrange("p (s k h w) -> p s k h w", s=2, k=6, h=H)
        o += 2 * n_v
        oT = region[:, o:o + 2 * n_o].rearrange("p (s g l t) -> p s g l t", s=2, g=G, l=2)
        n_w1 = NE * DFF
        assert 2 * n_w1 + NE * FC * D <= o + n_o
        w1 = [region[:, 0:n_w1], region[0:DL, n_w1:2 * n_w1]]
        w2 = region[:, 2 * n_w1:2 * n_w1 + NE * FC * D]

        psS = ctx.enter_context(nc.psum_tensor("psS", [P, 2, 2, 512], F32))
        psO = ctx.enter_context(nc.psum_tensor("psO", [P, 512], F32))
        ring = [ctx.enter_context(nc.psum_tensor(f"ring{i}", [P, 512], F32)) for i in range(R)]

        xs = nc.dram_tensor("slot_x", (SLOTS, D), F32, kind="Internal").ap()
        ys = nc.dram_tensor("slot_y", (SLOTS, D), F32, kind="Internal").ap()

        ld_cst, ld_img, ld_txt, ld_qkv, ld_mem, ld_out = (sem(n) for n in (
            "ld_cst", "ld_img", "ld_txt", "ld_qkv", "ld_mem", "ld_out"))
        ld_moe = sem("ld_moe")
        s_zero = sem("s_zero")
        s_ring = sem("s_ring")
        s_dr = {"A": sem("s_drain_act"), "D": sem("s_drain_dve")}
        s_chain = sem("s_chain")
        s_achain = sem("s_achain")
        s_const = sem("s_const")
        s_var, s_r0 = sem("s_var"), sem("s_r0")
        s_xn = sem("s_xn")
        s_split = sem("s_split")
        s_memsplit = sem("s_memsplit")
        s_neg = sem("s_neg")
        s_mrow = sem("s_mrow")
        s_moff = sem("s_moff")
        s_score, s_exp, s_value, s_keep = sem("s_score"), sem("s_exp"), sem("s_value"), sem("s_keep")
        s_att = sem("s_att")
        s_ln2 = sem("s_ln2")
        s_shift, s_p = sem("s_shift"), sem("s_p")
        s_hot = sem("s_hot")
        s_slot = sem("s_slot")
        s_scat = sem("s_scat")
        s_gath = [sem(f"s_gathered{k}") for k in range(4)]
        s_gfree = sem("s_gfree")
        s_x = [sem("s_slot_x_even"), sem("s_slot_x_odd")]
        s_mx, s_mxT = sem("s_slot_xT_ps"), sem("s_slot_xT")
        s_h, s_g, s_hTp, s_hT = sem("s_hidden"), sem("s_gelu"), sem("s_hiddenT_ps"), sem("s_hiddenT")
        s_y, s_ysb = sem("s_y"), sem("s_y_sbuf")
        s_yst = [sem("s_y_stored_even"), sem("s_y_stored_odd")]
        s_fin, s_out = sem("s_fin"), sem("s_out")

        mx_in = sb("mx_in", [P, 2, D])
        mxT = [sb("mxT_a", [P, 2, P]), sb("mxT_b", [DL, 2, P])]
        hg = sb("hg", [P, 2, DFF])
        hT = sb("hT", [P, 2, DFF])
        yb = sb("yb", [P, 2, D])
        oh = sb("oh", [P, 2, NT, NE])
        w8 = sb("w8", [P, NT, NE])
        w8b = sb("w8b", [P, NT, NE])
        m12 = sb("m12", [P, 2, NT])
        dd = sb("dd", [P, NT])
        gsum = sb("gsum", [P, NT])
        ginv = sb("ginv", [P, NT])
        gw = sb("gw", [P, 2, NT])
        spare = patchT[:].rearrange("p a b c -> p (a b c)")
        n_pre = 2 * (NT + 1) * NE
        pre = spare[:, 0:n_pre].rearrange("p (c i e) -> p c i e", c=2, e=NE)
        cmp = sb("cmp", [P, NE, EXP_TILES])
        nt_e = sb("nt_e", [P, NE])
        end = sb("end", [P, 2, NE])
        base = sb("base", [P, NE])
        posn = sb("posn", [P, NT, NE])
        slotf = sb("slotf", [P, 2, NT])
        slot = sb("slot", [P, 2, NT], U32)
        tcmp = spare[:, n_pre:n_pre + SLOT_TILES * NE].rearrange("p (t e) -> p t e", e=NE)
        texf = sb("texf", [P, SLOT_TILES])
        tex = sb("tex", [P, SLOT_TILES], I32)
        yg = pr[:].rearrange("p a b c -> p (a b c)")[:, 0:4 * 2 * D].rearrange("p (a b d) -> p a b d", a=4, b=2)
        zrow = sb("zrow", [P, SLOT_TILES * D // ZN])

        def bank(key):
            return ring[PLACE[key] % R]

        def job_free(eng, key):
            k = PLACE[key] - R
            if k >= 0:
                who, n = DRAINS[k]
                eng.wait_ge(s_dr[who], n)

        def job_done(eng, key):
            eng.wait_ge(s_ring, PLACE[key] + 1)

        def drained(eng, key):
            who, n = DRAINS[PLACE[key]]
            eng.wait_ge(s_dr[who], n)

        block = ctx.enter_context(nc.Block())

        @block.sync
        def _(sp):
            sp.dma_start(cst[:], a["cst"]).then_inc(ld_cst, 16)
            sp.dma_start(patchT[:], a["patchT"]).then_inc(ld_img, 16)
            sp.dma_start(tokw[:], a["tokw"]).then_inc(ld_img, 16)
            sp.dma_start(clsb[:], a["clsb"]).then_inc(ld_img, 16)
            sp.dma_start(pos[:], a["pos"]).then_inc(ld_img, 16)
            for b in range(B):
                sp.dma_start(h_all[:, b * TT:b * TT + TT - 1, :],
                             a["txt"][b].rearrange("(t p) d -> p t d", p=P)).then_inc(ld_txt, 16)
            for dst, src, s in ((wqkv, "wqkv", ld_qkv), (memT, "memT", ld_mem), (wmem, "wmem", ld_mem),
                                (wout, "wout", ld_out), (wr, "wr", ld_out)):
                last = dst[1].shape[0]
                sp.dma_start(dst[0][:], a[src][0:P, :]).then_inc(s, 16)
                sp.dma_start(dst[1][:], a[src][P:P + last, :]).then_inc(s, 16)
            sp.wait_ge(s_const, 1)
            for i in range(ZN):
                n = SLOTS // ZN
                sp.dma_start(xs[i * n:(i + 1) * n, :].rearrange("(p r) d -> p (r d)", p=P), zrow[:]).then_inc(s_zero, 16)
            for s in ORDER:
                if s[0] == "maxT":
                    g = s[1]
                    sp.wait_ge(s_mrow, g + 1)
                    for j in range(GH):
                        sp.dma_start(qst[KQ:KM, g // G % 2, (g % G) * GH + j, :],
                                     mrow[4 * j:4 * j + 4, :]).then_inc(s_moff, 16)
            sp.wait_ge(s_value, B * G * NC * TT)
            sp.wait_ge(s_att, (B - 1) * TT)
            for i in range(2):
                last = (P, DL)[i]
                sp.dma_start(w1[i].rearrange("p (e f) -> p e f", e=NE),
                             a["w1"][:, i * P:i * P + last, :].rearrange("e d f -> d e f")).then_inc(ld_moe, 16)
            sp.dma_start(w2.rearrange("p (e c d) -> p e c d", e=NE, c=FC),
                         a["w2"].rearrange("e (c p) d -> p e c d", p=P)).then_inc(ld_moe, 16)
            sp.wait_ge(s_scat, 16 * 2 * NT)
            for u in range(2):
                sp.dma_start(mx_in[:, u, :], xs[u * P:(u + 1) * P, :]).then_inc(s_x[u], 16)
            with sp.Fori(1, SLOT_TILES // 2) as pair:
                for u in range(2):
                    i = 2 * pair + u
                    sp.wait_ge(s_mx, i - 1)
                    sp.dma_start(mx_in[:, u, :], xs[bass.ds(i * P, P), :]).then_inc(s_x[u], 16)
            for i in range(NT):
                b, t = divmod(i, TT)
                sp.wait_ge(s_fin, i + 1)
                dst = out[b, NIMG + t * P:NIMG + (t + 1) * P, :] if t < TT - 1 else out[b, 0:NIMG, :]
                sp.dma_start(dst, h_all[0:rows_of(t), i, :]).then_inc(s_out, 16)
            sp.wait_ge(s_out, 16 * NT)

        @block.gpsimd
        def _(pool):
            fills = [(zrow[:], 0.0), (val, 0.0), (val[:, :, 0:TT - 1, :, HD:HD + 1], 1.0),
                     (val[0:NIMG, :, TT - 1:TT, :, HD:HD + 1], 1.0), (val[MEM:P, :, TT:TT + 1, :, HD:HD + 1], 1.0),
                     (xT[1][DL:DL + 1, :, :], 1.0), (ks[:, :, :, KQ:KM], 0.0), (mv[:], 1.0), (mx[:], 0.0),
                     (mt[:], 0.0), (logit[:], 0.0)]
            for k, (dst, v) in enumerate(fills):
                pool.memset(dst, v).then_inc(s_const, 1)
                pool.wait_ge(s_const, k + 1)
            pool.wait_ge(s_zero, 16 * ZN)
            pool.wait_ge(s_slot, 1)
            for i in range(NT):
                n = rows_of(i % TT)
                for c in range(TOPK):
                    pool.indirect_dma_start(
                        out=xs, out_offset=bass.IndirectOffsetOnAxis(ap=slot[0:n, c, i:i + 1], axis=0),
                        in_=xn[0:n, i, :], in_offset=None).then_inc(s_scat, 16)
            for u in range(2):
                pool.wait_ge(s_yst[u], 16 * SLOT_TILES // 2)
            for i in range(NT):
                n = rows_of(i % TT)
                if i >= 4:
                    pool.wait_ge(s_gfree, i - 3)
                for c in range(TOPK):
                    pool.indirect_dma_start(
                        out=yg[0:n, i % 4, c, :], out_offset=None, in_=ys,
                        in_offset=bass.IndirectOffsetOnAxis(ap=slot[0:n, c, i:i + 1], axis=0)).then_inc(s_gath[i % 4], 16)

        @block.scalar
        def _(act):
            def power(n0, n1, k):
                act.wait_ge(s_var, k)
                act.activation(lnv[:, n0:n1], ve[:, n0:n1], ACT.Ln).then_inc(s_achain, 1)
                act.wait_ge(s_achain, k)
                act.activation(r0[:, n0:n1], lnv[:, n0:n1], ACT.Exp, scale=-0.5).then_inc(s_r0, 1)

            def transposed(dst, key, buf, n):
                job_done(act, key)
                act.activation(dst[0][:, buf, 0:n], bank(key)[:, 0:n], ACT.Copy)
                act.activation(dst[1][0:DL, buf, 0:n], bank(key)[0:DL, P:P + n], ACT.Copy).then_inc(s_dr["A"], 1)

            act.wait_ge(s_const, 11)
            job_done(act, ("mem", 0))
            act.activation(qk[0:MEM, 0, D:2 * D], bank(("mem", 0))[0:MEM, 0:D], ACT.Copy).then_inc(s_dr["A"], 1)
            job_done(act, ("mem", 1))
            for sl in range(2):
                ins = act.activation(val[MEM:P, sl, TT, :, 0:HD],
                                     bank(("mem", 1))[MEM:P, 0:D].rearrange("p (h d) -> p h d", h=H), ACT.Copy)
            ins.then_inc(s_dr["A"], 1)
            power(0, NT, 1)
            for c, (h0, h1) in enumerate(((0, 8), (8, H))):
                key = ("memT", c)
                job_done(act, key)
                src = bank(key)[:].bitcast(BF16)[0:KM, 0:(h1 - h0) * P].rearrange("p (h t) -> p h t", t=P)
                for sl in range(2):
                    ins = act.activation(kst[0:KM, sl, h0:h1, KEYS - MEM:KEYS], src[:, :, 0:MEM], ACT.Copy)
                ins.then_inc(s_dr["A"], 1)

            for s in ORDER:
                kind = s[0]
                if kind in ("xT", "attT", "ln2T"):
                    i = s[1]
                    transposed(xT, s + (0,), i % 2, rows_of(i % TT))
                elif kind == "qkv":
                    i = s[1]
                    b, t = divmod(i, TT)
                    n = rows_of(t)
                    job_done(act, s + (0,))
                    if i >= 2:
                        act.wait_ge(s_split, i - 1)
                    else:
                        act.wait_ge(s_memsplit, 1)
                    act.activation(qk[0:n, i % 2, :], bank(s + (0,))[0:n, 0:2 * D], ACT.Copy).then_inc(s_dr["A"], 1)
                    job_done(act, s + (1,))
                    if b >= 2:
                        act.wait_ge(s_value, (b - 1) * G * NC * TT)
                    act.activation(val[0:n, b % 2, t, :, 0:HD],
                                   bank(s + (1,))[0:n, 0:D].rearrange("p (h d) -> p h d", h=H), ACT.Copy).then_inc(s_dr["A"], 1)
                elif kind == "stack":
                    i = s[1]
                    b, t = divmod(i, TT)
                    n = rows_of(t)
                    for c, (h0, h1) in enumerate(((0, 8), (8, H))):
                        job_done(act, s + (c,))
                        src = bank(s + (c,))[:].bitcast(BF16)[0:KQ, 0:(h1 - h0) * P].rearrange("p (h t) -> p h t", t=P)
                        if b >= 2:
                            act.wait_ge(s_score, (b - 1) * G * NC * TT)
                        act.activation(qst[0:KQ, b % 2, h0:h1, t * P:t * P + n], src[:, :, 0:n], ACT.Copy).then_inc(s_dr["A"], 1)
                elif kind == "maxT":
                    g = s[1]
                    job_done(act, s + (0,))
                    if g >= 1:
                        act.wait_ge(s_moff, 16 * GH * g)
                    act.activation(mrow[:, :], bank(s + (0,))[:].bitcast(BF16)[0:4 * GH, 0:T], ACT.Copy).then_inc(s_dr["A"], 1)
                    act.wait_ge(s_dr["A"], DRAINS[PLACE[s + (0,)]][1])
                    act.sem_inc(s_mrow, 1)
                elif kind == "score":
                    n = s[1]
                    act.wait_ge(s_score, n + 1)
                    if n >= 3:
                        act.wait_ge(s_value, n - 2)
                    act.activation(pr[:, n % 3], psS[:, n % 2, :, 0:2 * QC], ACT.Exp, scale=HD ** -0.5).then_inc(s_exp, 1)
                elif kind == "keep":
                    c = s[1]
                    g, q = divmod(c, NC)
                    b = g // G
                    act.wait_ge(s_value, (c + 1) * TT)
                    if b >= 2:
                        act.wait_ge(s_att, (b - 1) * TT)
                    act.activation(oT[:, b % 2, g % G, :, q * QC:(q + 1) * QC],
                                   psO[:, 0:2 * QC].rearrange("p (l q) -> p l q", l=2), ACT.Copy).then_inc(s_keep, 1)
                elif kind == "rstd":
                    power(s[1] * TT, (s[1] + 1) * TT, s[1] + 2)
            act.wait_ge(s_shift, 1)
            act.activation(w8b[:], w8[:], ACT.Exp).then_inc(s_p, 1)
            act.activation(gw[:, 1, :], dd[:], ACT.Exp).then_inc(s_p, 1)

            def hidden(i, cur):
                act.wait_ge(s_h, i + 1)
                act.wait_ge(s_hTp, i - 1) if not isinstance(i, int) or i >= 2 else None
                act.activation(hg[:, cur, :].rearrange("p (a f) -> p a f", a=2), psS[:, cur, :, 0:DFF // 2], ACT.Gelu_apprx_tanh).then_inc(s_g, 1)

            def result(i, cur, pair):
                act.wait_ge(s_y, i + 1)
                if not isinstance(pair, int) or pair >= 1:
                    act.wait_ge(s_yst[cur], 16 * pair)
                act.activation(yb[:, cur, :], psO[:, 0:D], ACT.Copy).then_inc(s_ysb, 1)
                act.wait_ge(s_ysb, i + 1)
                act.dma_start(ys[bass.ds(i * P, P), :], yb[:, cur, :]).then_inc(s_yst[cur], 16)

            hidden(0, 0)
            hidden(1, 1)
            result(0, 0, 0)
            hidden(2, 0)
            result(1, 1, 0)
            with act.Fori(1, SLOT_TILES // 2 - 1) as pair:
                i = 2 * pair
                hidden(i + 1, 1)
                result(i, 0, pair)
                hidden(i + 2, 0)
                result(i + 1, 1, pair)
            hidden(SLOT_TILES - 1, 1)
            result(SLOT_TILES - 2, 0, SLOT_TILES // 2 - 1)
            result(SLOT_TILES - 1, 1, SLOT_TILES // 2 - 1)

        @block.tensor
        def _(pe):
            def group(dst, pairs, **kw):
                for n, (l, r) in enumerate(pairs):
                    ins = pe.matmul(dst, l, r, start=(n == 0), stop=(n == len(pairs) - 1), **kw)
                return ins

            def transpose2(dst, src, n):
                pe.transpose(dst[:, 0:n], src[:, 0:P], ident[0:n, 0:n])
                return pe.transpose(dst[0:DL, P:P + n], src[:, P:D], ident[0:n, 0:n])

            pe.wait_ge(ld_cst, 16)
            pe.wait_ge(ld_img, 64)
            for c in range(2):
                key = ("img", c)
                job_free(pe, key)
                for b in range(2):
                    ins = group(bank(key)[0:NIMG, b * D:(b + 1) * D],
                                [(cst[0:2, C_SEL:C_SEL + NIMG], clsb[:])] +
                                [(patchT[:, k, 2 * c + b, :], tokw[:, k, :]) for k in range(PC)])
                ins.then_inc(s_ring, 1)
            pe.wait_ge(ld_mem, 64)
            for c, rows in enumerate((slice(0, MEM), slice(MEM, P))):
                key = ("mem", c)
                job_free(pe, key)
                group(bank(key)[rows, 0:D], [(memT[k][:], wmem[k][:]) for k in range(2)]).then_inc(s_ring, 1)
            pe.wait_ge(s_memsplit, 1)
            for c, (h0, h1) in enumerate(((0, 8), (8, H))):
                key = ("memT", c)
                job_free(pe, key)
                for h in range(h0, h1):
                    ins = pe.transpose(bank(key)[:].bitcast(BF16)[0:KM, (h - h0) * P:(h - h0) * P + MEM],
                                       ks[0:MEM, 0, h, :], identb[0:MEM, 0:MEM])
                ins.then_inc(s_ring, 1)
            pe.wait_ge(ld_qkv, 32)
            pe.wait_ge(ld_out, 64)

            for s in ORDER:
                kind = s[0]
                if JOBS.get(kind):
                    i = s[1]
                    b, t = divmod(i, TT)
                    n = rows_of(t)
                if kind == "xT":
                    pe.wait_ge(s_xn, i + 1)
                    job_free(pe, s + (0,))
                    transpose2(bank(s + (0,)), xn[0:n, i, :], n).then_inc(s_ring, 1)
                elif kind == "qkv":
                    drained(pe, ("xT", i, 0))
                    lhs = (xT[0][:, i % 2, 0:n], xT[1][:, i % 2, 0:n])
                    for c, (c0, c1) in enumerate(((0, 2 * D), (2 * D, 3 * D))):
                        job_free(pe, s + (c,))
                        group(bank(s + (c,))[0:n, 0:c1 - c0],
                              [(lhs[k], wqkv[k][:, c0:c1]) for k in range(2)]).then_inc(s_ring, 1)
                elif kind == "stack":
                    pe.wait_ge(s_split, i + 1)
                    for c in range(4):
                        job_free(pe, s + (c,))
                        src, rows = (qs, KQ) if c < 2 else (ks, KM)
                        h0, h1 = ((0, 8), (8, H))[c % 2]
                        dst = bank(s + (c,))[:].bitcast(BF16)
                        for h in range(h0, h1):
                            ins = pe.transpose(dst[0:rows, (h - h0) * P:(h - h0) * P + n],
                                               src[0:n, i % 2, h, :], identb[0:n, 0:n])
                        ins.then_inc(s_ring, 1)
                elif kind == "max":
                    _, g, t, j = s
                    n, sl = rows_of(t), g // G % 2
                    if t == 0 and j == 0:
                        for c in (1, 3):
                            drained(pe, ("stack", g // G * TT + TT - 1, c))
                    job_free(pe, s + (0,))
                    heads = [(g % G) * GH + j] if j < GH else [(g % G) * GH + x for x in range(GH)]
                    for x, h in enumerate(heads):
                        dst, k0, k1 = (slice(0, 512), 0, 512) if j < GH else (slice(x * P, x * P + P), 512, KEYS)
                        ins = pe.matmul(bank(s + (0,))[0:n, dst], qst[0:KQ, sl, h, t * P:t * P + n],
                                        kst[0:KQ, sl, h, k0:k1], start=True, stop=True)
                    ins.then_inc(s_ring, 1)
                elif kind == "maxT":
                    g = s[1]
                    pe.wait_ge(s_neg, g + 1)
                    job_free(pe, s + (0,))
                    for t in range(TT):
                        n = rows_of(t)
                        ins = pe.transpose(bank(s + (0,))[:].bitcast(BF16)[0:4 * GH, t * P:t * P + n],
                                           mp[0:n, g % 2, t].rearrange("p j c -> p (j c)"), identb[0:n, 0:n])
                    ins.then_inc(s_ring, 1)
                elif kind == "score":
                    n = s[1]
                    c, k = divmod(n, TT)
                    g, c = divmod(c, NC)
                    sl = g // G % 2
                    if c == 0 and k == 0:
                        pe.wait_ge(s_moff, 16 * GH * (g + 1))
                    if n >= 2:
                        pe.wait_ge(s_exp, n - 1)
                    for j in range(GH):
                        h = (g % G) * GH + j
                        ins = pe.matmul(psS[:, n % 2, j // 2, (j % 2) * QC:(j % 2 + 1) * QC],
                                        kst[0:KM, sl, h, k * P:(k + 1) * P],
                                        qst[0:KM, sl, h, c * QC:(c + 1) * QC], start=True, stop=True)
                    ins.then_inc(s_score, 1)
                elif kind == "value":
                    n = s[1]
                    c, k = divmod(n, TT)
                    g = c // NC
                    sl = g // G % 2
                    pe.wait_ge(s_exp, n + 1)
                    if k == 0 and c >= 1:
                        pe.wait_ge(s_keep, c)
                    for j in range(GH):
                        h = (g % G) * GH + j
                        rhs = pr[:, n % 3, j // 2, (j % 2) * QC:(j % 2 + 1) * QC]
                        ins = pe.matmul(psO[32 * j:32 * j + VW, 0:QC], val[:, sl, k, h, :], rhs,
                                        start=(k == 0), stop=(k == TT - 1))
                    if k == TT - 1:
                        for j in range(GH):
                            h = (g % G) * GH + j
                            rhs = pr[:, n % 3, j // 2, (j % 2) * QC:(j % 2 + 1) * QC]
                            ins = pe.matmul(psO[32 * j:32 * j + VW, QC:2 * QC], val[:, sl, TT, h, :], rhs,
                                            start=True, stop=True)
                    ins.then_inc(s_value, 1)
                elif kind == "norm":
                    if t == 0:
                        pe.wait_ge(s_keep, (b + 1) * G * NC)
                    for l in range(2):
                        job_free(pe, s + (l,))
                        for g in range(G):
                            ins = pe.transpose(bank(s + (l,))[0:n, g * P:(g + 1) * P],
                                               oT[:, b % 2, g, l, t * P:t * P + n], ident)
                        ins.then_inc(s_ring, 1)
                elif kind == "attT":
                    pe.wait_ge(s_att, i + 1)
                    job_free(pe, s + (0,))
                    transpose2(bank(s + (0,)), att[0:n, i % 2, :], n).then_inc(s_ring, 1)
                elif kind == "proj":
                    drained(pe, ("attT", i, 0))
                    job_free(pe, s + (0,))
                    group(bank(s + (0,))[0:n, 0:D], [(xT[k][:, i % 2, 0:n], wout[k][:]) for k in range(2)]).then_inc(s_ring, 1)
                elif kind == "ln2T":
                    pe.wait_ge(s_ln2, i + 1)
                    job_free(pe, s + (0,))
                    transpose2(bank(s + (0,)), xn[0:n, i, :], n).then_inc(s_ring, 1)
                elif kind == "router":
                    drained(pe, ("ln2T", i, 0))
                    job_free(pe, s + (0,))
                    group(bank(s + (0,))[0:n, 0:NE],
                          [(xT[0][:, i % 2, 0:n], wr[0][:]), (xT[1][0:DL, i % 2, 0:n], wr[1][:])]).then_inc(s_ring, 1)

            pe.wait_ge(s_hot, 1)
            for c, m in enumerate((tri, ones)):
                job_free(pe, ("rank", c))
                pe.matmul(bank(("rank", c))[:, 0:NT * NE], m, w8[:].rearrange("p i e -> p (i e)"),
                          start=True, stop=True).then_inc(s_ring, 1)

            def load_expert(i):
                return pe.value_load(tex[0:1, bass.ds(i, 1)], min_val=0, max_val=NE - 1)

            def slot_T(i, cur, pair):
                pe.wait_ge(s_x[cur], 16 * (pair + 1))
                pe.wait_ge(s_mxT, i) if not isinstance(i, int) or i >= 1 else None
                transpose2(ring[0], mx_in[:, cur, :], P).then_inc(s_mx, 1)

            def up(i, cur, half, e):
                if half == 0:
                    pe.wait_ge(s_mxT, i + 1)
                    pe.wait_ge(s_g, i - 1) if not isinstance(i, int) or i >= 2 else None
                w = DFF // 2
                for k in range(2):
                    ins = pe.matmul(psS[:, cur, half, 0:w], mxT[k][:, cur, :],
                                    w1[k][:, bass.ds(e * DFF + half * w, w)], start=(k == 0), stop=(k == 1))
                if half == 1:
                    ins.then_inc(s_h, 1)

            def hidden_T(i, cur):
                pe.wait_ge(s_g, i + 1)
                pe.wait_ge(s_hT, i) if not isinstance(i, int) or i >= 1 else None
                for c in range(FC):
                    ins = pe.transpose(ring[1 + c // 3][:, (c % 3) * P:(c % 3 + 1) * P], hg[:, cur, c * P:(c + 1) * P], ident)
                ins.then_inc(s_hTp, 1)

            def down(i, cur, e):
                pe.wait_ge(s_hT, i + 1)
                pe.wait_ge(s_ysb, i) if not isinstance(i, int) or i >= 1 else None
                for c in range(FC):
                    ins = pe.matmul(psO[:, 0:D], hT[:, cur, c * P:(c + 1) * P],
                                    w2[:, bass.ds((e * FC + c) * D, D)], start=(c == 0), stop=(c == FC - 1))
                ins.then_inc(s_y, 1)

            pe.wait_ge(s_slot, 1)
            pe.wait_ge(ld_moe, 48)
            for c in range(2):
                drained(pe, ("rank", c))
            slot_T(0, 0, 0)
            e0 = load_expert(0)
            up(0, 0, 0, e0)
            up(0, 0, 1, e0)
            slot_T(1, 1, 0)

            def item(i, cur):
                nxt = load_expert(i + 1)
                e = load_expert(i)
                up(i + 1, 1 - cur, 0, nxt)
                hidden_T(i, cur)
                up(i + 1, 1 - cur, 1, nxt)
                return e

            e = item(0, 0)
            slot_T(2, 0, 1)
            down(0, 0, e)
            e = item(1, 1)
            slot_T(3, 1, 1)
            down(1, 1, e)
            with pe.Fori(1, SLOT_TILES // 2 - 1) as pair:
                i = 2 * pair
                for u in range(2):
                    e = item(i + u, u)
                    slot_T(i + u + 2, u, pair + 1)
                    down(i + u, u, e)
            e = item(SLOT_TILES - 2, 0)
            down(SLOT_TILES - 2, 0, e)
            e = load_expert(SLOT_TILES - 1)
            hidden_T(SLOT_TILES - 1, 1)
            down(SLOT_TILES - 1, 1, e)

        @block.vector
        def _(dve):
            steps = [0]

            def link(ins):
                steps[0] += 1
                ins.then_inc(s_chain, 1)
                dve.wait_ge(s_chain, steps[0])

            def refine(n0, n1, k):
                v, r, t = ve[:, n0:n1], r0[:, n0:n1], rn[:, n0:n1]
                dve.wait_ge(s_r0, k)
                link(dve.tensor_tensor(t, r, r, ALU.mult))
                link(dve.tensor_tensor(t, t, v, ALU.mult))
                link(dve.tensor_scalar(t, t, -0.5, 1.5, ALU.mult, ALU.add))
                link(dve.tensor_tensor(rstd[:, n0:n1], t, r, ALU.mult))

            def normalise(i):
                n = rows_of(i % TT)
                return dve.tensor_scalar(xn[0:n, i, :], h_all[0:n, i, :], mv[0:n, i, 0:1], rstd[0:n, i:i + 1],
                                         ALU.subtract, ALU.mult)

            def moments(i):
                n = rows_of(i % TT)
                link(dve.bn_stats(stats[0:n, i, :], h_all[0:n, i, :]))
                dve.bn_aggr(mv[0:n, i, :], stats[0:n, i, :]).then_inc(s_chain, 1)
                steps[0] += 1

            def split(n, cols, buf, q, k):
                w = slice(cols, 2 * D)
                link(dve.tensor_copy(hi[0:n, w], qk[0:n, buf, w]))
                link(dve.tensor_tensor(rest[0:n, w], qk[0:n, buf, w], hi[0:n, w], ALU.subtract))
                link(dve.tensor_copy(mid[0:n, w], rest[0:n, w]))
                dve.tensor_tensor(ks[0:n, buf, :, 2 * HD:3 * HD], by_head(rest, n, D)[:, :, 0, :], by_head(mid, n, D)[:, :, 0, :], ALU.subtract)
                if q:
                    dve.tensor_tensor(qs[0:n, buf, :, 5 * HD:6 * HD], by_head(rest, n, 0)[:, :, 0, :], by_head(mid, n, 0)[:, :, 0, :], ALU.subtract)
                    dst = qs[0:n, buf].rearrange("p h (s d) -> p h s d", d=HD)
                    dve.tensor_copy(dst[:, :, 0:3, :], by_head(hi, n, 0).to_broadcast([n, H, 3, HD]))
                    dve.tensor_copy(dst[:, :, 3:5, :], by_head(mid, n, 0).to_broadcast([n, H, 2, HD]))
                dst = ks[0:n, buf, :, 0:KQ].rearrange("p h (s d) -> p h s d", d=HD)
                dve.tensor_copy(dst[:, :, 0:4:3, :], by_head(hi, n, D).to_broadcast([n, H, 2, HD]))
                dve.tensor_copy(dst[:, :, 5:6, :], by_head(hi, n, D))
                return dve.tensor_copy(dst[:, :, 1:5:3, :], by_head(mid, n, D).to_broadcast([n, H, 2, HD]))

            def by_head(x, n, c0):
                return x[0:n, c0:c0 + D].rearrange("p (h o d) -> p h o d", h=H, o=1)

            dve.wait_ge(ld_cst, 16)
            link(dve.tensor_copy(identb[:], ident))
            dve.wait_ge(s_const, 11)
            dve.wait_ge(ld_img, 64)
            for c in range(2):
                job_done(dve, ("img", c))
                for b in range(2):
                    ins = dve.tensor_tensor(h_all[0:NIMG, (2 * c + b) * TT + TT - 1, :],
                                            bank(("img", c))[0:NIMG, b * D:(b + 1) * D], pos[:], ALU.add)
                ins.then_inc(s_dr["D"], 1)
            dve.wait_ge(s_dr["D"], 2)
            dve.wait_ge(ld_txt, 16 * B)
            for i in range(NT):
                moments(i)
            dve.wait_ge(s_chain, steps[0])
            dve.tensor_scalar(ve[:], mv[:, :, 1], EPS, None, ALU.add).then_inc(s_var, 1)
            drained(dve, ("mem", 0))
            link(dve.memset(ks[0:MEM, 0, :, KQ + 2:KM], 1.0))
            link(split(MEM, D, 0, False, True))
            dve.sem_inc(s_memsplit, 1)
            refine(0, NT, 1)
            for i in range(TT):
                normalise(i).then_inc(s_xn, 1)
            drained(dve, ("memT", 0))
            drained(dve, ("memT", 1))
            link(dve.memset(ks[:, :, :, KQ:KQ + 2], 1.0))
            link(dve.memset(ks[:, :, :, KQ + 2:KM], 0.0))

            for s in ORDER:
                kind = s[0]
                i = s[1]
                b, t = divmod(i, TT)
                n = rows_of(t)
                if kind == "split":
                    drained(dve, ("qkv", i, 0))
                    if i >= 2:
                        drained(dve, ("stack", i - 2, 3))
                        dve.wait_ge(s_ring, PLACE[("stack", i - 2, 3)] + 1)
                    link(split(n, 0, i % 2, True, True))
                    dve.sem_inc(s_split, 1)
                elif kind == "stack":
                    for c, (h0, h1) in enumerate(((0, 8), (8, H))):
                        key = s + (c + 2,)
                        job_done(dve, key)
                        if b >= 2:
                            dve.wait_ge(s_score, (b - 1) * G * NC * TT)
                        src = bank(key)[:].bitcast(BF16)[0:KM, 0:(h1 - h0) * P].rearrange("p (h t) -> p h t", t=P)
                        ins = dve.tensor_copy(kst[0:KM, b % 2, h0:h1, t * P:t * P + n], src[:, :, 0:n])
                        if t == TT - 1:
                            ins = dve.tensor_copy(kst[0:KM, b % 2, h0:h1, t * P + n:KEYS - MEM], src[:, :, 0:KEYS - MEM - t * P - n])
                        ins.then_inc(s_dr["D"], 1)
                    if t == TT - 1 and b + 1 < B:
                        for x in range(TT):
                            normalise(i + 1 + x).then_inc(s_xn, 1)
                elif kind == "max":
                    _, g, t, j = s
                    n = rows_of(t)
                    job_done(dve, s + (0,))
                    if j < GH:
                        ins = dve.tensor_reduce(mx[0:n, g % 2, t, j:j + 1], bank(s + (0,))[0:n, :], AX, ALU.max)
                    else:
                        ins = dve.tensor_reduce(mt[0:n, g % 2, t], bank(s + (0,))[0:n, :].rearrange("p (j l k) -> p j l k", j=GH, l=2), AX, ALU.max)
                    ins.then_inc(s_dr["D"], 1)
                elif kind == "negmax":
                    g = s[1]
                    u = g % 2
                    drained(dve, ("max", g, TT - 1, GH, 0))
                    if g >= 2:
                        dve.wait_ge(s_ring, PLACE[("maxT", g - 2, 0)] + 1)
                    link(dve.tensor_tensor(mt[:, u, :, :, 0], mx[:, u], mt[:, u, :, :, 0], ALU.max))
                    m = mt[:, u].rearrange("p t j l -> p (t j) l")
                    parts = mp[:, u].rearrange("p t j (l c) -> p (t j) l c", c=2)
                    link(dve.tensor_scalar(parts[:, :, :, 0], m, -1.0, None, ALU.mult))
                    dve.scalar_tensor_tensor(out=parts[:, :, :, 1], in0=m, scalar=-1.0, in1=parts[:, :, :, 0],
                                             op0=ALU.mult, op1=ALU.subtract).then_inc(s_neg, 1)
                elif kind == "norm":
                    u = i % 2
                    for l in range(2):
                        job_done(dve, s + (l,))
                        src = bank(s + (l,))[0:n, 0:G * P].rearrange("p (g j w) -> p g j w", g=G, w=VW)
                        link(dve.reciprocal(rec[0:n, l], src[:, :, :, HD]))
                        r = rec[0:n, l].rearrange("p g (j o) -> p g j o", o=1).to_broadcast([n, G, GH, HD])
                        dve.tensor_tensor(prod[0:n, l], src[:, :, :, 0:HD], r, ALU.mult).then_inc(s_dr["D"], 1)
                    if i >= 2:
                        dve.wait_ge(s_ring, PLACE[("attT", i - 2, 0)] + 1)
                    drained(dve, s + (1,))
                    dve.tensor_tensor(att[0:n, u, :], prod[0:n, 0].rearrange("p g j d -> p (g j d)"),
                                      prod[0:n, 1].rearrange("p g j d -> p (g j d)"), ALU.add).then_inc(s_att, 1)
                    dve.wait_ge(s_att, i + 1)
                elif kind == "proj":
                    job_done(dve, s + (0,))
                    dve.tensor_tensor(h_all[0:n, i, :], bank(s + (0,))[0:n, 0:D], h_all[0:n, i, :], ALU.add).then_inc(s_dr["D"], 1)
                    drained(dve, s + (0,))
                    moments(i)
                elif kind == "rstd":
                    b = s[1]
                    dve.wait_ge(s_chain, steps[0])
                    dve.tensor_scalar(ve[:, b * TT:(b + 1) * TT], mv[:, b * TT:(b + 1) * TT, 1], EPS, None, ALU.add).then_inc(s_var, 1)
                    refine(b * TT, (b + 1) * TT, b + 2)
                elif kind == "ln2":
                    normalise(i).then_inc(s_ln2, 1)
                elif kind == "router":
                    job_done(dve, s + (0,))
                    dve.tensor_copy(logit[0:n, i, :], bank(s + (0,))[0:n, 0:NE]).then_inc(s_dr["D"], 1)

            drained(dve, ("router", NT - 1, 0))
            wide = lambda x: x.rearrange("p (i o) -> p i o", o=1).to_broadcast([P, NT, NE])
            pref = cst[:, C_PREF:C_PREF + NE].rearrange("p (o e) -> p o e", o=1).to_broadcast([P, NT, NE])
            work = logit
            for c in range(2):
                m = m12[:, c, :]
                link(dve.tensor_reduce(m, work[:], AX, ALU.max))
                link(dve.tensor_tensor(w8[:], work[:], wide(m), ALU.is_equal))
                link(dve.tensor_tensor(w8[:], w8[:], pref, ALU.mult))
                link(dve.tensor_reduce(dd[:], w8[:], AX, ALU.max))
                link(dve.tensor_tensor(oh[:, c], w8[:], wide(dd[:]), ALU.is_equal))
                if c == 0:
                    link(dve.tensor_scalar(w8b[:], oh[:, 0], -3.0e38, None, ALU.mult))
                    link(dve.tensor_tensor(posn[:], logit[:], w8b[:], ALU.add))
                    work = posn
            link(dve.tensor_tensor(w8[:], logit[:], wide(m12[:, 0, :]), ALU.subtract))
            link(dve.tensor_tensor(dd[:], m12[:, 1, :], m12[:, 0, :], ALU.subtract))
            dve.sem_inc(s_shift, 1)
            dve.wait_ge(s_p, 2)
            link(dve.tensor_reduce(gsum[:], w8b[:], AX, ALU.add))
            link(dve.reciprocal(gw[:, 0, :], gsum[:]))
            link(dve.tensor_tensor(gw[:, 1, :], gw[:, 1, :], gw[:, 0, :], ALU.mult))
            valid = cst[:, C_VALID:C_VALID + NT]
            for c in range(2):
                link(dve.tensor_tensor(oh[:, c], oh[:, c], wide(valid), ALU.mult))
            dve.tensor_tensor(w8[:], oh[:, 0], oh[:, 1], ALU.add).then_inc(s_hot, 1)
            job_done(dve, ("rank", 0))
            job_done(dve, ("rank", 1))
            rank = bank(("rank", 0))[:, 0:NT * NE].rearrange("p (i e) -> p i e", e=NE)
            total = bank(("rank", 1))[:, 0:NT * NE].rearrange("p (i e) -> p i e", e=NE)
            link(dve.memset(pre[:, :, 0:1, :], 0.0))
            link(dve.tensor_copy(pre[:, 0, 1:NT + 1, :], total))
            cur, step = 0, 1
            while step < NT:
                dve.tensor_copy(pre[:, 1 - cur, 1:1 + step, :], pre[:, cur, 1:1 + step, :]).then_inc(s_chain, 1)
                steps[0] += 1
                link(dve.tensor_tensor(pre[:, 1 - cur, 1 + step:NT + 1, :], pre[:, cur, 1 + step:NT + 1, :],
                                       pre[:, cur, 1:NT + 1 - step, :], ALU.add))
                cur, step = 1 - cur, 2 * step
            count = pre[:, cur, NT:NT + 1, :].rearrange("p o e -> p e o").to_broadcast([P, NE, EXP_TILES])
            kk = cst[:, C_K:C_K + EXP_TILES].rearrange("p (o k) -> p o k", o=1).to_broadcast([P, NE, EXP_TILES])
            link(dve.tensor_tensor(cmp[:], count, kk, ALU.is_gt))
            link(dve.tensor_reduce(nt_e[:], cmp[:], AX, ALU.add))
            link(dve.tensor_copy(end[:, 0, :], nt_e[:]))
            u, step = 0, 1
            while step < NE:
                dve.tensor_copy(end[:, 1 - u, 0:step], end[:, u, 0:step]).then_inc(s_chain, 1)
                steps[0] += 1
                link(dve.tensor_tensor(end[:, 1 - u, step:NE], end[:, u, step:NE], end[:, u, 0:NE - step], ALU.add))
                u, step = 1 - u, 2 * step
            link(dve.tensor_tensor(base[:], end[:, u, :], nt_e[:], ALU.subtract))
            link(dve.tensor_scalar(base[:], base[:], float(P), None, ALU.mult))
            link(dve.tensor_tensor(posn[:], rank, pre[:, cur, 0:NT, :], ALU.add))
            link(dve.tensor_tensor(posn[:], posn[:], base[:].rearrange("p (o e) -> p o e", o=1).to_broadcast([P, NT, NE]), ALU.add))
            for c in range(2):
                link(dve.tensor_tensor(w8b[:], oh[:, c], posn[:], ALU.mult))
                link(dve.tensor_reduce(slotf[:, c, :], w8b[:], AX, ALU.add))
            link(dve.tensor_copy(slot[:], slotf[:]))
            tau = cst[:, C_TAU:C_TAU + SLOT_TILES].rearrange("p (t o) -> p t o", o=1).to_broadcast([P, SLOT_TILES, NE])
            ends = end[:, u, :].rearrange("p (o e) -> p o e", o=1).to_broadcast([P, SLOT_TILES, NE])
            link(dve.tensor_tensor(tcmp, tau, ends, ALU.is_ge))
            link(dve.tensor_reduce(texf[:], tcmp, AX, ALU.add))
            link(dve.tensor_scalar(texf[:], texf[:], float(NE - 1), None, ALU.min))
            link(dve.tensor_copy(tex[:], texf[:]))
            dve.sem_inc(s_dr["D"], 2)
            dve.sem_inc(s_slot, 1)

            def slot_T(i, cur):
                dve.wait_ge(s_mx, i + 1)
                dve.wait_ge(s_h, i - 1) if not isinstance(i, int) or i >= 2 else None
                dve.tensor_copy(mxT[0][:, cur, :], ring[0][:, 0:P])
                dve.tensor_copy(mxT[1][:, cur, :], ring[0][0:DL, P:2 * P]).then_inc(s_mxT, 1)

            def hidden_T(i, cur):
                dve.wait_ge(s_hTp, i + 1)
                dve.wait_ge(s_y, i - 1) if not isinstance(i, int) or i >= 2 else None
                dve.tensor_copy(hT[:, cur, 0:3 * P], ring[1][:, 0:3 * P])
                dve.tensor_copy(hT[:, cur, 3 * P:6 * P], ring[2][:, 0:3 * P]).then_inc(s_hT, 1)

            slot_T(0, 0)
            slot_T(1, 1)
            hidden_T(0, 0)
            slot_T(2, 0)
            hidden_T(1, 1)
            slot_T(3, 1)
            with dve.Fori(1, SLOT_TILES // 2 - 1) as pair:
                i = 2 * pair
                hidden_T(i, 0)
                slot_T(i + 2, 0)
                hidden_T(i + 1, 1)
                slot_T(i + 3, 1)
            hidden_T(SLOT_TILES - 2, 0)
            hidden_T(SLOT_TILES - 1, 1)

            for i in range(NT):
                n = rows_of(i % TT)
                dve.wait_ge(s_gath[i % 4], 32 * (i // 4 + 1))
                for c in range(2):
                    ins = dve.scalar_tensor_tensor(out=h_all[0:n, i, :], in0=yg[0:n, i % 4, c, :], scalar=gw[0:n, c, i:i + 1],
                                                   in1=h_all[0:n, i, :], op0=ALU.mult, op1=ALU.add)
                    if c == 0:
                        link(ins)
                ins.then_inc(s_fin, 1)
                dve.wait_ge(s_fin, i + 1)
                dve.sem_inc(s_gfree, 1)


def kernel(x, txt, L0_tok_W, L0_tok_b, L0_tok_class_token, L0_tok_pos_embedding, L0_attn_w_qkv, L0_attn_b_qkv,
           L0_attn_w_out, L0_attn_b_out, L0_attn_w_mem, L0_attn_b_mem, L0_attn_memory, L0_ffn_router_w,
           L0_ffn_w1, L0_ffn_w2):
    import numpy as np
    import concourse.bacc as bacc
    from concourse.bass_utils import run_bass_kernel_spmd

    f = lambda v: np.asarray(v)
    s = 16
    n = 96 // s
    x = f(x)
    pt = x.reshape(B, 3, n, s, n, s).transpose(0, 1, 2, 4, 3, 5).reshape(B, NPATCH, PD).transpose(2, 0, 1)
    patchT = np.zeros((PC, P, B, NIMG), x.dtype)
    patchT[:, :, :, 1:] = pt.reshape(PC, P, B, NPATCH)
    with_row = lambda w, row: np.concatenate([w, row.reshape(1, -1)], 0)
    cst = np.zeros((P, C_N), np.float32)
    cst[:, C_ID:C_ID + P] = np.eye(P)
    cst[:, C_TRI:C_TRI + P] = np.triu(np.ones((P, P)), 1)
    cst[:, C_ONE:C_ONE + P] = 1
    cst[:, C_PREF:C_PREF + NE] = NE - np.arange(NE)
    cst[:, C_TAU:C_TAU + SLOT_TILES] = np.arange(SLOT_TILES)
    cst[:, C_K:C_K + EXP_TILES] = P * np.arange(EXP_TILES)
    for i in range(NT):
        cst[0:rows_of(i % TT), C_VALID + i] = 1
    cst[0, C_SEL] = 1
    cst[1, C_SEL + 1:C_SEL + NIMG] = 1
    mem = f(L0_attn_memory)[0]
    arrays = {
        "cst": cst,
        "patchT": patchT.transpose(1, 0, 2, 3),
        "tokw": f(L0_tok_W).T.reshape(PC, P, D).transpose(1, 0, 2),
        "clsb": np.concatenate([f(L0_tok_class_token), f(L0_tok_b).reshape(1, -1)], 0),
        "pos": f(L0_tok_pos_embedding),
        "txt": f(txt),
        "wqkv": with_row(f(L0_attn_w_qkv), f(L0_attn_b_qkv)),
        "wout": with_row(f(L0_attn_w_out), f(L0_attn_b_out)),
        "wmem": with_row(f(L0_attn_w_mem), f(L0_attn_b_mem)),
        "memT": with_row(mem.T, np.ones(MEM, mem.dtype)),
        "wr": f(L0_ffn_router_w).T,
        "w1": f(L0_ffn_w1),
        "w2": f(L0_ffn_w2),
    }
    nc = bacc.Bacc("TRN2", target_bir_lowering=False, num_devices=1)
    ins, aps = {}, {}
    for name, v in arrays.items():
        v = np.ascontiguousarray(v)
        ins["in_" + name] = v
        aps[name] = nc.dram_tensor("in_" + name, v.shape, mybir.dt.from_np(v.dtype), kind="ExternalInput").ap()
    out = nc.dram_tensor("out", (B, T, D), F32, kind="ExternalOutput").ap()
    build(nc, aps, out)
    r = run_bass_kernel_spmd(nc, [ins], core_ids=[0])
    return r.results[0]["out"]
```

```python
from contextlib import ExitStack

import concourse.bass as bass
from concourse import mybir
from concourse.alu_op_type import AluOpType as ALU

F32 = mybir.dt.float32
BF16 = mybir.dt.bfloat16
U32 = mybir.dt.uint32
I32 = mybir.dt.int32
F32R = mybir.dt.float32r
ACT = mybir.ActivationFunctionType
AX = mybir.AxisListType.X

P = 128
B = 4
D = 192
DL = D - P
H, HD = 12, 16
NPATCH = 36
NIMG = NPATCH + 1
NTXT = 512
T = NIMG + NTXT
TT = 5
NT = B * TT
PD = 768
PC = PD // P
MEM = 64
GH = 4
G = H // GH
KQ = 6 * HD
KM = KQ + 4
KEYS = 5 * P
QC = 183
NC = T // QC
VW = 32
NE, DFF, TOPK = 8, 768, 2
FC = DFF // P
SLOT_TILES = (B * T * TOPK + NE * (P - 1)) // P
SLOTS = SLOT_TILES * P
EXP_TILES = (B * T + P - 1) // P
EPS = 1e-5
NROWS = B * T + P
HOTS = 10
SW = 1536
HALVES = ((0, 8), (8, H))
R = 3

C_ID, C_TRI, C_ONE = 0, P, 2 * P
C_PREF = 3 * P
C_TAU = C_PREF + NE
C_K = C_TAU + SLOT_TILES
C_VALID = C_K + EXP_TILES
C_SEL = C_VALID + NT
C_ROW = C_SEL + NIMG
C_EMPTY = C_ROW + NT
C_COL = C_EMPTY + 1
C_N = C_COL + P


def rows_of(t):
    return P if t < TT - 1 else NIMG


def weight_chunks():
    cuts = lambda n: [(c, min(SW, n - c)) for c in range(0, n, SW)]
    return [(w, c, n) for w, total in (("w1a", NE * DFF), ("w1b", NE * DFF), ("w2", NE * FC * D))
            for c, n in cuts(total)]


CHUNKS = weight_chunks()
EARLY = 4


PHASE = 0.4
WORK = {"xT": 0.3, "qk": 1.3, "v": 0.7, "split": 0.65, "stack": 1.1, "max": 0.8, "norm": 0.8, "attT": 0.3, "proj": 1.4,
        "rstd": 2.0, "ln2": 0.3, "ln2T": 0.3, "router": 0.4, "whi": 2.0, "wload": 0.5}


def plan():
    front = lambda b: [s for t in range(TT + 2) for s in (
        ([("xT", b * TT + t)] if t < TT else []) +
        ([("qk", b * TT + t), ("v", b * TT + t)] + [("split", b * TT + t, x) for x in range(4)] if t < TT else []) +
        ([("stack", b * TT + t - 1, x) for x in range(4)] if 1 <= t <= TT else []))]
    maxima = lambda g: [("max", g, t, j) for t in range(TT) for j in range(GH + 1)] + [("negmax", g)]
    merge = lambda b: [s for t in range(TT + 2) for s in (
        ([("norm", b * TT + t, l) for l in range(2)] if t < TT else []) +
        ([("attT", b * TT + t - 1)] if 1 <= t <= TT else []) +
        ([("proj", b * TT + t - 2)] if 2 <= t else []))]
    gate = lambda b: [("rstd", b)] + [s for t in range(TT + 2) for s in (
        ([("ln2", b * TT + t)] if t < TT else []) +
        ([("ln2T", b * TT + t - 1)] if 1 <= t <= TT else []) +
        ([("router", b * TT + t - 2)] if 2 <= t else []))]
    units, NG = TT * NC, B * G
    fill = []

    def spread(stages, start, end):
        cost = [WORK.get(s[0], 0.1) for s in stages]
        done = 0.0
        for s, c in zip(stages, cost):
            fill.append((start + (end - start) * (done + c / 2) / sum(cost), len(fill), s))
            done += c

    for g in range(1, NG):
        spread(maxima(g), units * (g - 2 + PHASE), units * (g - 1 + PHASE))
        fill.append((units * (g - 1 + PHASE) + 2, len(fill), ("maxT", g)))
    for b in range(B):
        at = b * G * units
        if b + 1 < B:
            spread(front(b + 1), at, at + units * (1 + PHASE) * 0.95)
        if b > 0:
            spread(merge(b - 1) + gate(b - 1), at + (units * (1 + PHASE) if b + 1 < B else 0), at + G * units)
    w = list(range(EARLY))
    early = [("wload", k) for k in w[:2]]
    for k in w:
        early += [("whi", k)] + ([("wload", k + 2)] if k + 2 in w else [])
    early += [("wload", EARLY), ("wload", EARLY + 1)]
    spread(early, (NG - G) * units + 1, NG * units)
    fill.sort()
    order = front(0) + maxima(0) + [("maxT", 0)]
    for n in range(NG * units):
        if n % units == 0:
            if n == 0:
                order += [s for x, _, s in fill if x < 0]
            order.append(("score", n))
        if (n + 1) % units:
            order.append(("score", n + 1))
        order += [s for x, _, s in fill if n <= x < n + 1]
        order.append(("value", n))
        if n % TT == TT - 1:
            order.append(("keep", n // TT))
    late = [[("whi", k)] + ([("wload", k + 2)] if k + 2 < len(CHUNKS) else []) for k in range(EARLY, len(CHUNKS))]
    order += sum(late[0:2], []) + merge(B - 1) + sum(late[2:4], []) + gate(B - 1)
    order += sum(late[4:5], []) + [("gates",)] + sum(late[5:], [])
    return order


ORDER = plan()
JOBS = {"img": "DD", "mem": "AA", "memT": "AA", "xT": "A", "qk": "A", "v": "A", "stack": "A", "max": "D",
        "maxT": "A", "norm": "D", "attT": "A", "proj": "D", "ln2T": "A", "router": "D", "rank": "DD"}


def ring_plan():
    place, drains, count = {}, [], {"A": 0, "D": 0}
    for s in [("img",), ("mem",), ("memT",)] + ORDER + [("rank",)]:
        for part, who in enumerate("AADD"[s[2]] if s[0] == "stack" else JOBS.get(s[0], "")):
            count[who] += 1
            place[s + (part,)] = len(drains)
            drains.append((who, count[who]))
    return place, drains


PLACE, DRAINS = ring_plan()


def build(nc, a, out):
    ctx = ExitStack()
    sb = lambda name, shape, dt=F32: ctx.enter_context(nc.sbuf_tensor(name, shape, dt))
    sem = lambda name: ctx.enter_context(nc.semaphore(name))
    with ctx:
        cst = sb("cst", [P, C_N])
        ident, tri, ones = cst[:, C_ID:C_ID + P], cst[:, C_TRI:C_TRI + P], cst[:, C_ONE:C_ONE + P]
        identb = sb("identb", [P, P], BF16)
        top = lambda name, shape, dt=F32: nc.sbuf_tensor(name, shape, dt, side="right")
        with top("rows", [P, 2, NT, D]) as rows:
            h_all, xn = rows[:, 0], rows[:, 1]
        with top("hot", [P, 2, HOTS, P], F32R) as hot, top("sel", [P, 2, HOTS, 3, SLOT_TILES], F32R) as sel:
            pass
        mx_in = ctx.enter_context(top("mx_in", [P, 2, 2 * P]))
        xh = ctx.enter_context(top("xh", [P, 2, 2 * P], F32R))
        xl = ctx.enter_context(top("xl", [P, 2, 2 * P], F32R))
        yb = ctx.enter_context(top("yb", [P, 2, D]))
        hg = ctx.enter_context(top("hg", [P, 2, DFF]))
        hTh = ctx.enter_context(top("hTh", [P, 2, DFF], F32R))
        hTl = ctx.enter_context(top("hTl", [P, 2, DFF], F32R))
        ysum = ctx.enter_context(top("ysum", [P, 2, D]))
        last_rows = 2 * (2 * D + 6 * P + 3 * DFF)
        ctx.enter_context(top("rows_rest", [P, 2 * NT * D - last_rows]))
        wout = [sb("wout_a", [P, D]), sb("wout_b", [DL + 1, D])]
        wr = [sb("wr_a", [P, NE]), sb("wr_b", [DL, NE])]
        stats = sb("stats", [P, NT, 6])
        mv = sb("mv", [P, NT, 2])
        ve = sb("ve", [P, NT])
        lnv = sb("lnv", [P, NT])
        r0 = sb("r0", [P, NT])
        rn = sb("rn", [P, NT])
        rstd = sb("rstd", [P, NT])
        xT = [sb("xT_a", [P, 2, P]), sb("xT_b", [DL + 1, 2, P])]
        logit = sb("logit", [P, NT, NE])
        with ExitStack() as first:
            fsb = lambda name, shape: first.enter_context(nc.sbuf_tensor(name, shape, F32))
            patchT = fsb("patchT", [P, PC, B, NIMG])
            tokw = fsb("tokw", [P, PC, D])
            clsb = fsb("clsb", [2, D])
            pos = fsb("pos", [NIMG, D])
            wmem = [fsb("wmem_a", [P, D]), fsb("wmem_b", [DL + 1, D])]
            memT = [fsb("memT_a", [P, MEM]), fsb("memT_b", [DL + 1, MEM])]
            wqkv = [fsb("wqkv_a", [P, 3 * D]), fsb("wqkv_b", [DL + 1, 3 * D])]
        oh = sb("oh", [P, 2, NT, NE])
        w8 = sb("w8", [P, NT, NE])
        w8b = sb("w8b", [P, NT, NE])
        posn = sb("posn", [P, NT, NE])
        both = sb("both", [P, NT, NE])
        m12 = sb("m12", [P, 2, NT])
        dd = sb("dd", [P, NT])
        gsum = sb("gsum", [P, NT])
        gw = sb("gw", [P, 2, NT])
        pre = sb("pre", [P, 2, NT + 1, NE])
        cmp = sb("cmp", [P, NE, EXP_TILES])
        nt_e = sb("nt_e", [P, NE])
        end = sb("end", [P, 2, NE])
        base = sb("base", [P, NE])
        slotf = sb("slotf", [P, 2, NT])
        slot = sb("slot", [P, 2, NT], I32)
        within_i = sb("within_i", [P, 2, NT], I32)
        tile_i = sb("tile_i", [P, 2, NT], I32)
        within = sb("within", [P, 2, NT])
        tile = sb("tile", [P, 2, NT])
        weights = sb("weights", [P, 2, NT, 3], F32R)
        at = sb("at", [P, HOTS, SLOT_TILES])
        tcmp = sb("tcmp", [P, SLOT_TILES, NE])
        texf = sb("texf", [P, SLOT_TILES])
        tex = sb("tex", [P, SLOT_TILES], I32)
        row1 = sb("row1", [P, SLOT_TILES])
        rowf = sb("rowf", [P, SLOT_TILES])
        row = sb("row", [P, SLOT_TILES], U32)
        gate_of = sb("gate_of", [P, SLOT_TILES])
        stage = sb("stage", [P, 2, SW])

        with ExitStack() as attention:
            asb = lambda name, shape, dt=F32: attention.enter_context(nc.sbuf_tensor(name, shape, dt))
            qst, kst, val = [], [], []
            for sl in range(2):
                qst.append(asb(f"qst{sl}", [P, H, T], BF16))
                kst.append(asb(f"kst{sl}", [P, H, KEYS], BF16))
                val.append(asb(f"val{sl}", [P, 6, H, VW]))
                if sl == 0:
                    qk = asb("qk", [P, 2, 2 * D])
                    hi = asb("hi", [P, 2 * D], BF16)
                    mid = asb("mid", [P, 2 * D], BF16)
                    rest = asb("rest", [P, 2 * D])
                    qs = asb("qs", [P, 2, H, KQ], BF16)
                    ks = asb("ks", [P, 2, H, KM], BF16)
            mx = asb("mx", [P, 2, TT, GH])
            mt = asb("mt", [P, 2, TT, GH, 2])
            mp = asb("mp", [P, 2, TT, GH, 4], BF16)
            mrow = asb("mrow", [4 * GH, T], BF16)
            pr = asb("pr", [P, 3, 2, 2 * QC])
            oT = asb("oT", [P, 2, G, 2, T])
            rec = asb("rec", [P, 2, G, GH])
            prod = asb("prod", [P, 2, G, GH, HD])
            att = asb("att", [P, 2, D])
        w1a = [sb("w1a_high", [P, NE * DFF], F32R), sb("w1a_low", [P, NE * DFF], F32R)]
        w1b = sb("w1b", [P, NE * DFF], F32R)
        w2 = sb("w2", [P, NE * FC, 2, D], F32R)

        psS = ctx.enter_context(nc.psum_tensor("psS", [P, 2, 2, 512], F32))
        psO = ctx.enter_context(nc.psum_tensor("psO", [P, 512], F32))
        rings = ctx.enter_context(nc.psum_tensor("rings", [P, R, 512], F32))
        ring = [rings[:, i, :] for i in range(R)]

        xrow = nc.dram_tensor("normalised", (NROWS, 2 * P), F32, kind="Internal").ap()

        ld_cst, ld_img, ld_txt, ld_qkv, ld_mem, ld_out = (sem(n) for n in (
            "ld_cst", "ld_img", "ld_txt", "ld_qkv", "ld_mem", "ld_out"))
        ld_w = [sem("ld_weights_even"), sem("ld_weights_odd")]
        s_whi, s_wlo = sem("s_weights_high"), sem("s_weights_low")
        s_hst, s_xst = sem("s_residual_stored"), sem("s_normalised_stored")
        s_ring = sem("s_ring")
        s_dr = {"A": sem("s_drain_act"), "D": sem("s_drain_dve")}
        s_chain = sem("s_chain")
        s_achain = sem("s_achain")
        s_const = sem("s_const")
        s_var, s_r0 = sem("s_var"), sem("s_r0")
        s_xn = sem("s_xn")
        s_split = sem("s_split")
        s_memsplit = sem("s_memsplit")
        s_neg = sem("s_neg")
        s_mrow = sem("s_mrow")
        s_moff = sem("s_moff")
        s_score, s_exp, s_value, s_keep = sem("s_score"), sem("s_exp"), sem("s_value"), sem("s_keep")
        s_att = sem("s_att")
        s_ln2 = sem("s_ln2")
        s_shift, s_p = sem("s_shift"), sem("s_p")
        s_hot = sem("s_hot")
        s_onehot = sem("s_onehot")
        s_list = sem("s_list")
        s_route = sem("s_route")
        s_half = sem("s_y_half")
        s_xh = sem("s_slot_xT_high")
        s_x = [sem("s_slot_x_even"), sem("s_slot_x_odd")]
        s_mx, s_mxT = sem("s_slot_xT_ps"), sem("s_slot_xT")
        s_h, s_g, s_hTp = sem("s_hidden"), sem("s_gelu"), sem("s_hiddenT_ps")
        s_hThi, s_hT = sem("s_hiddenT_high"), sem("s_hiddenT")
        s_y, s_ysum, s_ysb = sem("s_y"), sem("s_y_sum"), sem("s_y_sbuf")
        s_acc = sem("s_accumulated")

        W = DFF // 2
        N_CONST = 14

        def bank(key):
            return ring[PLACE[key] % R]

        def job_free(eng, key):
            k = PLACE[key] - R
            if k >= 0:
                who, n = DRAINS[k]
                eng.wait_ge(s_dr[who], n)

        def job_done(eng, key):
            eng.wait_ge(s_ring, PLACE[key] + 1)

        def drained(eng, key):
            who, n = DRAINS[PLACE[key]]
            eng.wait_ge(s_dr[who], n)

        block = ctx.enter_context(nc.Block())

        @block.sync
        def _(sp):
            sp.dma_start(cst[:], a["cst"]).then_inc(ld_cst, 16)
            sp.dma_start(patchT[:], a["patchT"]).then_inc(ld_img, 16)
            sp.dma_start(tokw[:], a["tokw"]).then_inc(ld_img, 16)
            sp.dma_start(clsb[:], a["clsb"]).then_inc(ld_img, 16)
            sp.dma_start(pos[:], a["pos"]).then_inc(ld_img, 16)
            for b in range(B):
                sp.dma_start(h_all[:, b * TT:b * TT + TT - 1, :],
                             a["txt"][b].rearrange("(t p) d -> p t d", p=P)).then_inc(ld_txt, 16)
            for dst, src, s in ((wqkv, "wqkv", ld_qkv), (memT, "memT", ld_mem), (wmem, "wmem", ld_mem),
                                (wout, "wout", ld_out), (wr, "wr", ld_out)):
                last = dst[1].shape[0]
                sp.dma_start(dst[0][:], a[src][0:P, :]).then_inc(s, 16)
                sp.dma_start(dst[1][:], a[src][P:P + last, :]).then_inc(s, 16)
            sp.wait_ge(ld_cst, 16)
            for dst, width, done in ((out, D, s_hst), (xrow, 2 * P, s_xst)):
                sp.dma_start(dst[B * T:NROWS, :], cst[:, 0:width]).then_inc(done, 16)
            for s in ORDER:
                if s[0] == "maxT":
                    g = s[1]
                    sp.wait_ge(s_mrow, g + 1)
                    for j in range(GH):
                        sp.dma_start(qst[g // G % 2][KQ:KM, (g % G) * GH + j, :],
                                     mrow[4 * j:4 * j + 4, :]).then_inc(s_moff, 16)
                elif s[0] == "ln2":
                    i = s[1]
                    b, t = divmod(i, TT)
                    n = rows_of(t)
                    r = b * T + (NIMG + t * P if t < TT - 1 else 0)
                    sp.wait_ge(s_ln2, i + 1)
                    sp.dma_start(out[r:r + n, :], h_all[0:n, i, :]).then_inc(s_hst, 16)
                    sp.dma_start(xrow[r:r + n, 0:D], xn[0:n, i, :]).then_inc(s_xst, 16)
                    sp.dma_start(xrow[r:r + n, D:2 * P], xn[0:n, i, P:D]).then_inc(s_xst, 16)
                elif s[0] == "wload":
                    k = s[1]
                    w, c, n = CHUNKS[k]
                    if k >= 2:
                        sp.wait_ge(s_wlo, k - 1)
                    if w == "w1b":
                        for half in range(2):
                            sp.dma_start(stage[half * DL:(half + 1) * DL, k % 2, 0:n],
                                         a["w1"][P:D, c:c + n]).then_inc(ld_w[k % 2], 16)
                    else:
                        src = a["w1"][0:P, c:c + n] if w == "w1a" else a["w2"][:, c:c + n]
                        sp.dma_start(stage[:, k % 2, 0:n], src).then_inc(ld_w[k % 2], 16)

        @block.gpsimd
        def _(pool):
            fills = [f for v in val for f in (
                (v[:], 0.0), (v[:, 0:TT - 1, :, HD:HD + 1], 1.0),
                (v[0:NIMG, TT - 1:TT, :, HD:HD + 1], 1.0), (v[MEM:P, TT:TT + 1, :, HD:HD + 1], 1.0))] + [
                     (xT[1][DL:DL + 1, :, :], 1.0), (ks[:, :, :, KQ:KM], 0.0), (mv[:], 1.0), (mx[:], 0.0),
                     (mt[:], 0.0), (logit[:], 0.0)]
            for k, (dst, v) in enumerate(fills):
                pool.memset(dst, v).then_inc(s_const, 1)
                pool.wait_ge(s_const, k + 1)
            for s in ORDER:
                if s[0] == "whi":
                    k = s[1]
                    w, c, n = CHUNKS[k]
                    pool.wait_ge(s_whi, k + 1)
                    if w == "w1b":
                        ins = pool.tensor_tensor(w1b[DL:P, c:c + n], stage[DL:P, k % 2, 0:n], w1b[DL:P, c:c + n], ALU.subtract)
                    elif w == "w1a":
                        ins = pool.tensor_tensor(w1a[1][:, c:c + n], stage[:, k % 2, 0:n], w1a[0][:, c:c + n], ALU.subtract)
                    else:
                        block = w2[:, c // D:(c + n) // D]
                        ins = pool.tensor_tensor(block[:, :, 1, :], stage[:, k % 2, 0:n].rearrange("p (x d) -> p x d", d=D),
                                                 block[:, :, 0, :], ALU.subtract)
                    ins.then_inc(s_wlo, 1)
                    pool.wait_ge(s_wlo, k + 1)

            def gather(i):
                pool.indirect_dma_start(
                    out=mx_in[:, i % 2, :], out_offset=None, in_=xrow,
                    in_offset=bass.IndirectOffsetOnAxis(ap=row[:, i:i + 1], axis=0)).then_inc(s_x[i % 2], 16)

            pool.wait_ge(s_xst, 16 * (2 * NT + 1))
            pool.wait_ge(s_route, 1)
            for i in range(4):
                if i >= 2:
                    pool.wait_ge(s_mx, i - 1)
                gather(i)
            for i in range(SLOT_TILES):
                if i + 4 < SLOT_TILES:
                    pool.wait_ge(s_mx, i + 3)
                    gather(i + 4)
                pool.wait_ge(s_ysb, i + 1)
                if i == 0:
                    pool.wait_ge(s_hst, 16 * (NT + 1))
                else:
                    pool.wait_ge(s_acc, 16 * i)
                pool.indirect_dma_start(
                    out=out, out_offset=bass.IndirectOffsetOnAxis(ap=row[:, i:i + 1], axis=0),
                    in_=yb[:, i % 2, :], in_offset=None, compute_op=ALU.add).then_inc(s_acc, 16)
            pool.wait_ge(s_acc, 16 * SLOT_TILES)

        @block.scalar
        def _(act):
            def power(n0, n1, k):
                act.wait_ge(s_var, k)
                act.activation(lnv[:, n0:n1], ve[:, n0:n1], ACT.Ln).then_inc(s_achain, 1)
                act.wait_ge(s_achain, k)
                act.activation(r0[:, n0:n1], lnv[:, n0:n1], ACT.Exp, scale=-0.5).then_inc(s_r0, 1)

            def transposed(dst, key, buf, n):
                job_done(act, key)
                act.activation(dst[0][:, buf, 0:n], bank(key)[:, 0:n], ACT.Copy)
                act.activation(dst[1][0:DL, buf, 0:n], bank(key)[0:DL, P:P + n], ACT.Copy).then_inc(s_dr["A"], 1)

            act.wait_ge(s_const, N_CONST)
            job_done(act, ("mem", 0))
            act.activation(qk[0:MEM, 0, D:2 * D], bank(("mem", 0))[0:MEM, 0:D], ACT.Copy).then_inc(s_dr["A"], 1)
            job_done(act, ("mem", 1))
            for sl in range(2):
                ins = act.activation(val[sl][MEM:P, TT, :, 0:HD],
                                     bank(("mem", 1))[MEM:P, 0:D].rearrange("p (h d) -> p h d", h=H), ACT.Copy)
            ins.then_inc(s_dr["A"], 1)
            power(0, NT, 1)
            for c, (h0, h1) in enumerate(((0, 8), (8, H))):
                key = ("memT", c)
                job_done(act, key)
                src = bank(key)[:].bitcast(BF16)[0:KM, 0:(h1 - h0) * P].rearrange("p (h t) -> p h t", t=P)
                for sl in range(2):
                    ins = act.activation(kst[sl][0:KM, h0:h1, KEYS - MEM:KEYS], src[:, :, 0:MEM], ACT.Copy)
                ins.then_inc(s_dr["A"], 1)

            for s in ORDER:
                kind = s[0]
                if kind in ("xT", "attT", "ln2T"):
                    i = s[1]
                    transposed(xT, s + (0,), i % 2, rows_of(i % TT))
                elif kind == "qk":
                    i = s[1]
                    n = rows_of(i % TT)
                    job_done(act, s + (0,))
                    if i >= 2:
                        act.wait_ge(s_split, 4 * (i - 2) + 1)
                    else:
                        act.wait_ge(s_memsplit, 1)
                    act.activation(qk[0:n, i % 2, :], bank(s + (0,))[0:n, 0:2 * D], ACT.Copy).then_inc(s_dr["A"], 1)
                elif kind == "v":
                    b, t = divmod(s[1], TT)
                    n = rows_of(t)
                    job_done(act, s + (0,))
                    if b >= 2:
                        act.wait_ge(s_value, (b - 1) * G * NC * TT)
                    act.activation(val[b % 2][0:n, t, :, 0:HD],
                                   bank(s + (0,))[0:n, 0:D].rearrange("p (h d) -> p h d", h=H), ACT.Copy).then_inc(s_dr["A"], 1)
                elif kind == "stack" and s[2] < 2:
                    b, t = divmod(s[1], TT)
                    n = rows_of(t)
                    h0, h1 = HALVES[s[2]]
                    job_done(act, s + (0,))
                    src = bank(s + (0,))[:].bitcast(BF16)[0:KQ, 0:(h1 - h0) * P].rearrange("p (h t) -> p h t", t=P)
                    if b >= 2:
                        act.wait_ge(s_score, (b - 1) * G * NC * TT)
                    act.activation(qst[b % 2][0:KQ, h0:h1, t * P:t * P + n], src[:, :, 0:n], ACT.Copy).then_inc(s_dr["A"], 1)
                elif kind == "maxT":
                    g = s[1]
                    job_done(act, s + (0,))
                    if g >= 1:
                        act.wait_ge(s_moff, 16 * GH * g)
                    act.activation(mrow[:, :], bank(s + (0,))[:].bitcast(BF16)[0:4 * GH, 0:T], ACT.Copy).then_inc(s_dr["A"], 1)
                    act.wait_ge(s_dr["A"], DRAINS[PLACE[s + (0,)]][1])
                    act.sem_inc(s_mrow, 1)
                elif kind == "score":
                    n = s[1]
                    act.wait_ge(s_score, n + 1)
                    if n >= 3:
                        act.wait_ge(s_value, n - 2)
                    act.activation(pr[:, n % 3], psS[:, n % 2, :, 0:2 * QC], ACT.Exp, scale=HD ** -0.5).then_inc(s_exp, 1)
                elif kind == "keep":
                    c = s[1]
                    g, q = divmod(c, NC)
                    b = g // G
                    act.wait_ge(s_value, (c + 1) * TT)
                    if b >= 2:
                        act.wait_ge(s_att, (b - 1) * TT)
                    act.activation(oT[:, b % 2, g % G, :, q * QC:(q + 1) * QC],
                                   psO[:, 0:2 * QC].rearrange("p (l q) -> p l q", l=2), ACT.Copy).then_inc(s_keep, 1)
                elif kind == "gates":
                    act.wait_ge(s_shift, 2)
                    act.activation(w8b[:], w8[:], ACT.Exp).then_inc(s_p, 1)
                    act.activation(gw[:, 1, :], dd[:], ACT.Exp).then_inc(s_p, 1)
                elif kind == "whi":
                    k = s[1]
                    w, c, n = CHUNKS[k]
                    act.wait_ge(ld_w[k % 2], 16 * sum(2 if CHUNKS[x][0] == "w1b" else 1 for x in range(k % 2, k + 1, 2)))
                    if k == 0:
                        act.wait_ge(s_value, (B - 1) * G * NC * TT)
                        act.wait_ge(s_split, 4 * NT)
                        drained(act, ("stack", NT - 1, 3, 0))
                    elif k == EARLY:
                        act.wait_ge(s_value, B * G * NC * TT)
                    elif k == len(CHUNKS) - 2:
                        job_done(act, ("attT", NT - 1, 0))
                    if w == "w2":
                        act.activation(w2[:, c // D:(c + n) // D, 0, :],
                                       stage[:, k % 2, 0:n].rearrange("p (x d) -> p x d", d=D), ACT.Copy).then_inc(s_whi, 1)
                    else:
                        dst = w1a[0] if w == "w1a" else w1b
                        act.activation(dst[:, c:c + n], stage[:, k % 2, 0:n], ACT.Copy).then_inc(s_whi, 1)
                elif kind == "rstd":
                    power(s[1] * TT, (s[1] + 1) * TT, s[1] + 2)
            def gelu(i, cur):
                act.wait_ge(s_h, i + 1)
                act.wait_ge(s_hTp, i - 1) if not isinstance(i, int) or i >= 2 else None
                act.activation(hg[:, cur, :].rearrange("p (a f) -> p a f", a=2), psS[:, cur, :, 0:W], ACT.Gelu_apprx_tanh).then_inc(s_g, 1)

            def high(i, cur):
                act.wait_ge(s_hTp, i + 1)
                act.wait_ge(s_y, i - 1) if not isinstance(i, int) or i >= 2 else None
                for half in range(2):
                    act.activation(hTh[:, cur, half * W:(half + 1) * W], ring[1 + half][:, 0:W], ACT.Copy).then_inc(s_hThi, 1)

            def result(i, cur):
                act.wait_ge(s_ysum, i + 1)
                act.wait_ge(s_acc, 16 * i - 16) if not isinstance(i, int) or i >= 2 else None
                act.activation(yb[:, cur, :], ysum[:, cur, :], ACT.Copy, scale=gate_of[:, bass.ds(i, 1)]).then_inc(s_ysb, 1)

            def item(i, cur):
                high(i, cur)
                if not isinstance(i, int) or i >= 1:
                    result(i - 1, 1 - cur)
                if not isinstance(i, int) or i + 1 < SLOT_TILES:
                    gelu(i + 1, 1 - cur)

            gelu(0, 0)
            for i in range(4):
                item(i, i % 2)
            with act.Fori(2, SLOT_TILES // 2 - 1) as pair:
                for u in range(2):
                    item(2 * pair + u, u)
            for i in range(SLOT_TILES - 2, SLOT_TILES):
                item(i, i % 2)
            result(SLOT_TILES - 1, 1)

        @block.tensor
        def _(pe):
            def group(dst, pairs, **kw):
                for n, (l, r) in enumerate(pairs):
                    ins = pe.matmul(dst, l, r, start=(n == 0), stop=(n == len(pairs) - 1), **kw)
                return ins

            def transpose2(dst, src, n):
                pe.transpose(dst[:, 0:n], src[:, 0:P], ident[0:n, 0:n])
                return pe.transpose(dst[0:DL, P:P + n], src[:, P:D], ident[0:n, 0:n])

            pe.wait_ge(ld_cst, 16)
            pe.wait_ge(ld_img, 64)
            for c in range(2):
                key = ("img", c)
                job_free(pe, key)
                for b in range(2):
                    ins = group(bank(key)[0:NIMG, b * D:(b + 1) * D],
                                [(cst[0:2, C_SEL:C_SEL + NIMG], clsb[:])] +
                                [(patchT[:, k, 2 * c + b, :], tokw[:, k, :]) for k in range(PC)])
                ins.then_inc(s_ring, 1)
            pe.wait_ge(ld_mem, 64)
            for c, rows in enumerate((slice(0, MEM), slice(MEM, P))):
                key = ("mem", c)
                job_free(pe, key)
                group(bank(key)[rows, 0:D], [(memT[k][:], wmem[k][:]) for k in range(2)]).then_inc(s_ring, 1)
            pe.wait_ge(s_memsplit, 1)
            for c, (h0, h1) in enumerate(((0, 8), (8, H))):
                key = ("memT", c)
                job_free(pe, key)
                for h in range(h0, h1):
                    ins = pe.transpose(bank(key)[:].bitcast(BF16)[0:KM, (h - h0) * P:(h - h0) * P + MEM],
                                       ks[0:MEM, 0, h, :], identb[0:MEM, 0:MEM])
                ins.then_inc(s_ring, 1)
            pe.wait_ge(ld_qkv, 32)
            pe.wait_ge(ld_out, 64)

            for s in ORDER:
                kind = s[0]
                if JOBS.get(kind):
                    i = s[1]
                    b, t = divmod(i, TT)
                    n = rows_of(t)
                if kind == "xT":
                    pe.wait_ge(s_xn, i + 1)
                    job_free(pe, s + (0,))
                    transpose2(bank(s + (0,)), xn[0:n, i, :], n).then_inc(s_ring, 1)
                elif kind in ("qk", "v"):
                    drained(pe, ("xT", i, 0))
                    lhs = (xT[0][:, i % 2, 0:n], xT[1][:, i % 2, 0:n])
                    c0, c1 = (0, 2 * D) if kind == "qk" else (2 * D, 3 * D)
                    job_free(pe, s + (0,))
                    group(bank(s + (0,))[0:n, 0:c1 - c0],
                          [(lhs[k], wqkv[k][:, c0:c1]) for k in range(2)]).then_inc(s_ring, 1)
                elif kind == "stack":
                    pe.wait_ge(s_split, 4 * i + (3 if s[2] < 2 else 4))
                    job_free(pe, s + (0,))
                    src, rows_s = (qs, KQ) if s[2] < 2 else (ks, KM)
                    h0, h1 = HALVES[s[2] % 2]
                    dst = bank(s + (0,))[:].bitcast(BF16)
                    for h in range(h0, h1):
                        ins = pe.transpose(dst[0:rows_s, (h - h0) * P:(h - h0) * P + n],
                                           src[0:n, i % 2, h, :], identb[0:n, 0:n])
                    ins.then_inc(s_ring, 1)
                elif kind == "max":
                    _, g, t, j = s
                    n, sl = rows_of(t), g // G % 2
                    if t == 0 and j == 0:
                        for c in (1, 3):
                            drained(pe, ("stack", g // G * TT + TT - 1, c, 0))
                    job_free(pe, s + (0,))
                    heads = [(g % G) * GH + j] if j < GH else [(g % G) * GH + x for x in range(GH)]
                    for x, h in enumerate(heads):
                        dst, k0, k1 = (slice(0, 512), 0, 512) if j < GH else (slice(x * P, x * P + P), 512, KEYS)
                        ins = pe.matmul(bank(s + (0,))[0:n, dst], qst[sl][0:KQ, h, t * P:t * P + n],
                                        kst[sl][0:KQ, h, k0:k1], start=True, stop=True)
                    ins.then_inc(s_ring, 1)
                elif kind == "maxT":
                    g = s[1]
                    pe.wait_ge(s_neg, g + 1)
                    job_free(pe, s + (0,))
                    for t in range(TT):
                        n = rows_of(t)
                        ins = pe.transpose(bank(s + (0,))[:].bitcast(BF16)[0:4 * GH, t * P:t * P + n],
                                           mp[0:n, g % 2, t].rearrange("p j c -> p (j c)"), identb[0:n, 0:n])
                    ins.then_inc(s_ring, 1)
                elif kind == "score":
                    n = s[1]
                    c, k = divmod(n, TT)
                    g, c = divmod(c, NC)
                    sl = g // G % 2
                    if c == 0 and k == 0:
                        pe.wait_ge(s_moff, 16 * GH * (g + 1))
                    if n >= 2:
                        pe.wait_ge(s_exp, n - 1)
                    for j in range(GH):
                        h = (g % G) * GH + j
                        ins = pe.matmul(psS[:, n % 2, j // 2, (j % 2) * QC:(j % 2 + 1) * QC],
                                        kst[sl][0:KM, h, k * P:(k + 1) * P],
                                        qst[sl][0:KM, h, c * QC:(c + 1) * QC], start=True, stop=True)
                    ins.then_inc(s_score, 1)
                elif kind == "value":
                    n = s[1]
                    c, k = divmod(n, TT)
                    g = c // NC
                    sl = g // G % 2
                    pe.wait_ge(s_exp, n + 1)
                    if k == 0 and c >= 1:
                        pe.wait_ge(s_keep, c)
                    for j in range(GH):
                        h = (g % G) * GH + j
                        rhs = pr[:, n % 3, j // 2, (j % 2) * QC:(j % 2 + 1) * QC]
                        ins = pe.matmul(psO[32 * j:32 * j + VW, 0:QC], val[sl][:, k, h, :], rhs,
                                        start=(k == 0), stop=(k == TT - 1))
                    if k == TT - 1:
                        for j in range(GH):
                            h = (g % G) * GH + j
                            rhs = pr[:, n % 3, j // 2, (j % 2) * QC:(j % 2 + 1) * QC]
                            ins = pe.matmul(psO[32 * j:32 * j + VW, QC:2 * QC], val[sl][:, TT, h, :], rhs,
                                            start=True, stop=True)
                    ins.then_inc(s_value, 1)
                elif kind == "norm":
                    l = s[2]
                    if t == 0:
                        pe.wait_ge(s_keep, (b + 1) * G * NC)
                    job_free(pe, s + (0,))
                    for g in range(G):
                        ins = pe.transpose(bank(s + (0,))[0:n, g * P:(g + 1) * P],
                                           oT[:, b % 2, g, l, t * P:t * P + n], ident)
                    ins.then_inc(s_ring, 1)
                elif kind == "attT":
                    pe.wait_ge(s_att, i + 1)
                    job_free(pe, s + (0,))
                    transpose2(bank(s + (0,)), att[0:n, i % 2, :], n).then_inc(s_ring, 1)
                elif kind == "proj":
                    drained(pe, ("attT", i, 0))
                    job_free(pe, s + (0,))
                    group(bank(s + (0,))[0:n, 0:D], [(xT[k][:, i % 2, 0:n], wout[k][:]) for k in range(2)]).then_inc(s_ring, 1)
                elif kind == "ln2T":
                    pe.wait_ge(s_ln2, i + 1)
                    job_free(pe, s + (0,))
                    transpose2(bank(s + (0,)), xn[0:n, i, :], n).then_inc(s_ring, 1)
                elif kind == "router":
                    drained(pe, ("ln2T", i, 0))
                    job_free(pe, s + (0,))
                    group(bank(s + (0,))[0:n, 0:NE],
                          [(xT[0][:, i % 2, 0:n], wr[0][:]), (xT[1][0:DL, i % 2, 0:n], wr[1][:])]).then_inc(s_ring, 1)

            pe.wait_ge(s_hot, 1)
            for c, m in enumerate((tri, ones)):
                job_free(pe, ("rank", c))
                pe.matmul(bank(("rank", c))[:, 0:NT * NE], m, both[:].rearrange("p i e -> p (i e)"),
                          start=True, stop=True).then_inc(s_ring, 1)

            pe.wait_ge(s_keep, B * G * NC)
            for q in range(2 * NT // HOTS):
                pe.wait_ge(s_onehot, q + 1)
                for j in range(HOTS):
                    ins = pe.matmul(psO[:, 0:3 * SLOT_TILES], hot[:, q % 2, j, :], sel[:, q % 2, j].rearrange("p c t -> p (c t)"),
                                    start=(q + j == 0), stop=(q == 2 * NT // HOTS - 1 and j == HOTS - 1))
                ins.then_inc(s_list, 1)

            def load_expert(i):
                return pe.value_load(tex[0:1, bass.ds(i, 1)], min_val=0, max_val=NE - 1)

            def slot_T(i, cur, pair, down_next=False):
                pe.wait_ge(s_mxT, 1) if isinstance(i, int) and i == 1 else None
                pe.wait_ge(s_x[cur], 16 * (pair + 1))
                pe.transpose(ring[0][:, 0:P], mx_in[:, cur, 0:P], ident)
                if down_next:
                    pe.wait_ge(s_hT, 2 * i - 3)
                pe.transpose(ring[0][:, P:2 * P], mx_in[:, cur, P:2 * P], ident).then_inc(s_mx, 1)

            def up(i, cur, e):
                pe.wait_ge(s_mxT, i + 1)
                for half in range(2):
                    cols = bass.ds(e * DFF + half * W, W)
                    ins = group(psS[:, cur, half, 0:W],
                                [(xh[:, cur, 0:P], w1a[0][:, cols]), (xl[:, cur, 0:P], w1a[0][:, cols]),
                                 (xh[:, cur, 0:P], w1a[1][:, cols]),
                                 (xh[:, cur, P:2 * P], w1b[:, cols]), (xl[0:DL, cur, P:2 * P], w1b[0:DL, cols])])
                ins.then_inc(s_h, 1)

            def hidden_T(i, cur):
                pe.wait_ge(s_g, i + 1)
                for c in range(FC):
                    ins = pe.transpose(ring[1 + c // 3][:, (c % 3) * P:(c % 3 + 1) * P], hg[:, cur, c * P:(c + 1) * P], ident)
                ins.then_inc(s_hTp, 1)

            def down(i, cur, e):
                for c in range(FC):
                    if c == FC // 2:
                        pe.wait_ge(s_hT, 2 * i + 2)
                    block, rows_c = bass.ds(e * FC + c, 1), slice(c * P, (c + 1) * P)
                    wide = (psO[:, 0:2 * D], hTh[:, cur, rows_c], w2[:, block].rearrange("p x l d -> p (x l d)"))
                    narrow = (psO[:, 0:D], hTl[:, cur, rows_c], w2[:, block, 0, :].rearrange("p x d -> p (x d)"))
                    for x in ((wide, narrow) if c == 0 else (narrow, wide)):
                        ins = pe.matmul(*x, start=(c == 0 and x is wide), stop=(c == FC - 1 and x is wide))
                ins.then_inc(s_y, 1)

            pe.wait_ge(s_route, 1)
            pe.wait_ge(s_wlo, len(CHUNKS))
            for c in range(2):
                drained(pe, ("rank", c))
            slot_T(0, 0, 0)
            up(0, 0, load_expert(0))
            slot_T(1, 1, 0)
            hidden_T(0, 0)
            up(1, 1, load_expert(1))
            with pe.Fori(0, SLOT_TILES // 2 - 1) as pair:
                for u in range(2):
                    i = 2 * pair + u
                    e, e2 = load_expert(i), load_expert(i + 2)
                    slot_T(i + 2, u, pair + 1, True)
                    down(i, u, e)
                    hidden_T(i + 1, 1 - u)
                    up(i + 2, u, e2)
            for i in range(SLOT_TILES - 2, SLOT_TILES):
                e = load_expert(i)
                pe.wait_ge(s_hT, 2 * i + 1)
                down(i, i % 2, e)
                if i == SLOT_TILES - 2:
                    hidden_T(i + 1, 1)

        @block.vector
        def _(dve):
            steps = [0]

            def link(ins):
                steps[0] += 1
                ins.then_inc(s_chain, 1)
                dve.wait_ge(s_chain, steps[0])

            def refine(n0, n1, k):
                v, r, t = ve[:, n0:n1], r0[:, n0:n1], rn[:, n0:n1]
                dve.wait_ge(s_r0, k)
                link(dve.tensor_tensor(t, r, r, ALU.mult))
                link(dve.tensor_tensor(t, t, v, ALU.mult))
                link(dve.tensor_scalar(t, t, -0.5, 1.5, ALU.mult, ALU.add))
                link(dve.tensor_tensor(rstd[:, n0:n1], t, r, ALU.mult))

            def normalise(i):
                n = rows_of(i % TT)
                return dve.tensor_scalar(xn[0:n, i, :], h_all[0:n, i, :], mv[0:n, i, 0:1], rstd[0:n, i:i + 1],
                                         ALU.subtract, ALU.mult)

            def moments(i):
                n = rows_of(i % TT)
                link(dve.bn_stats(stats[0:n, i, :], h_all[0:n, i, :]))
                dve.bn_aggr(mv[0:n, i, :], stats[0:n, i, :]).then_inc(s_chain, 1)
                steps[0] += 1

            def split(step, n, cols, buf):
                w = slice(cols, 2 * D)
                if step == 0:
                    link(dve.tensor_copy(hi[0:n, w], qk[0:n, buf, w]))
                    return dve.tensor_tensor(rest[0:n, w], qk[0:n, buf, w], hi[0:n, w], ALU.subtract)
                if step == 1:
                    link(dve.tensor_copy(mid[0:n, w], rest[0:n, w]))
                    if cols == 0:
                        dve.tensor_tensor(qs[0:n, buf, :, 5 * HD:6 * HD], by_head(rest, n, 0)[:, :, 0, :], by_head(mid, n, 0)[:, :, 0, :], ALU.subtract)
                    return dve.tensor_tensor(ks[0:n, buf, :, 2 * HD:3 * HD], by_head(rest, n, D)[:, :, 0, :], by_head(mid, n, D)[:, :, 0, :], ALU.subtract)
                if step == 2:
                    dst = qs[0:n, buf].rearrange("p h (s d) -> p h s d", d=HD)
                    dve.tensor_copy(dst[:, :, 0:3, :], by_head(hi, n, 0).to_broadcast([n, H, 3, HD]))
                    return dve.tensor_copy(dst[:, :, 3:5, :], by_head(mid, n, 0).to_broadcast([n, H, 2, HD]))
                dst = ks[0:n, buf, :, 0:KQ].rearrange("p h (s d) -> p h s d", d=HD)
                dve.tensor_copy(dst[:, :, 0:4:3, :], by_head(hi, n, D).to_broadcast([n, H, 2, HD]))
                dve.tensor_copy(dst[:, :, 5:6, :], by_head(hi, n, D))
                return dve.tensor_copy(dst[:, :, 1:5:3, :], by_head(mid, n, D).to_broadcast([n, H, 2, HD]))

            def by_head(x, n, c0):
                return x[0:n, c0:c0 + D].rearrange("p (h o d) -> p h o d", h=H, o=1)

            dve.wait_ge(ld_cst, 16)
            link(dve.tensor_copy(identb[:], ident))
            dve.wait_ge(s_const, N_CONST)
            dve.wait_ge(ld_img, 64)
            for c in range(2):
                job_done(dve, ("img", c))
                for b in range(2):
                    ins = dve.tensor_tensor(h_all[0:NIMG, (2 * c + b) * TT + TT - 1, :],
                                            bank(("img", c))[0:NIMG, b * D:(b + 1) * D], pos[:], ALU.add)
                ins.then_inc(s_dr["D"], 1)
            dve.wait_ge(s_dr["D"], 2)
            dve.wait_ge(ld_txt, 16 * B)
            for i in range(NT):
                moments(i)
            dve.wait_ge(s_chain, steps[0])
            dve.tensor_scalar(ve[:], mv[:, :, 1], EPS, None, ALU.add).then_inc(s_var, 1)
            drained(dve, ("mem", 0))
            link(dve.memset(ks[0:MEM, 0, :, KQ + 2:KM], 1.0))
            for step in (0, 1, 3):
                link(split(step, MEM, D, 0))
            dve.sem_inc(s_memsplit, 1)
            refine(0, NT, 1)
            for i in range(TT):
                normalise(i).then_inc(s_xn, 1)
            drained(dve, ("memT", 0))
            drained(dve, ("memT", 1))
            link(dve.memset(ks[:, :, :, KQ:KQ + 2], 1.0))
            link(dve.memset(ks[:, :, :, KQ + 2:KM], 0.0))

            for s in ORDER:
                kind = s[0]
                if kind in ("gates", "wload", "whi"):
                    continue
                i = s[1]
                b, t = divmod(i, TT)
                n = rows_of(t)
                if kind == "split":
                    if s[2] == 0:
                        drained(dve, ("qk", i, 0))
                    elif s[2] == 1 and i >= 2:
                        dve.wait_ge(s_ring, PLACE[("stack", i - 2, 3, 0)] + 1)
                    link(split(s[2], n, 0, i % 2))
                    dve.sem_inc(s_split, 1)
                elif kind == "stack" and s[2] >= 2:
                    h0, h1 = HALVES[s[2] - 2]
                    key = s + (0,)
                    job_done(dve, key)
                    if b >= 2:
                        dve.wait_ge(s_score, (b - 1) * G * NC * TT)
                    src = bank(key)[:].bitcast(BF16)[0:KM, 0:(h1 - h0) * P].rearrange("p (h t) -> p h t", t=P)
                    ins = dve.tensor_copy(kst[b % 2][0:KM, h0:h1, t * P:t * P + n], src[:, :, 0:n])
                    if t == TT - 1:
                        ins = dve.tensor_copy(kst[b % 2][0:KM, h0:h1, t * P + n:KEYS - MEM], src[:, :, 0:KEYS - MEM - t * P - n])
                    ins.then_inc(s_dr["D"], 1)
                    if s[2] == 3 and b + 1 < B:
                        normalise(i + TT).then_inc(s_xn, 1)
                elif kind == "max":
                    _, g, t, j = s
                    n = rows_of(t)
                    job_done(dve, s + (0,))
                    if j < GH:
                        ins = dve.tensor_reduce(mx[0:n, g % 2, t, j:j + 1], bank(s + (0,))[0:n, :], AX, ALU.max)
                    else:
                        ins = dve.tensor_reduce(mt[0:n, g % 2, t], bank(s + (0,))[0:n, :].rearrange("p (j l k) -> p j l k", j=GH, l=2), AX, ALU.max)
                    ins.then_inc(s_dr["D"], 1)
                elif kind == "negmax":
                    g = s[1]
                    u = g % 2
                    drained(dve, ("max", g, TT - 1, GH, 0))
                    if g >= 2:
                        dve.wait_ge(s_ring, PLACE[("maxT", g - 2, 0)] + 1)
                    link(dve.tensor_tensor(mt[:, u, :, :, 0], mx[:, u], mt[:, u, :, :, 0], ALU.max))
                    m = mt[:, u].rearrange("p t j l -> p (t j) l")
                    parts = mp[:, u].rearrange("p t j (l c) -> p (t j) l c", c=2)
                    link(dve.tensor_scalar(parts[:, :, :, 0], m, -1.0, None, ALU.mult))
                    dve.scalar_tensor_tensor(out=parts[:, :, :, 1], in0=m, scalar=-1.0, in1=parts[:, :, :, 0],
                                             op0=ALU.mult, op1=ALU.subtract).then_inc(s_neg, 1)
                elif kind == "norm":
                    u, l = i % 2, s[2]
                    job_done(dve, s + (0,))
                    src = bank(s + (0,))[0:n, 0:G * P].rearrange("p (g j w) -> p g j w", g=G, w=VW)
                    link(dve.reciprocal(rec[0:n, l], src[:, :, :, HD]))
                    r = rec[0:n, l].rearrange("p g (j o) -> p g j o", o=1).to_broadcast([n, G, GH, HD])
                    dve.tensor_tensor(prod[0:n, l], src[:, :, :, 0:HD], r, ALU.mult).then_inc(s_dr["D"], 1)
                    if l == 0:
                        continue
                    if i >= 2:
                        dve.wait_ge(s_ring, PLACE[("attT", i - 2, 0)] + 1)
                    drained(dve, s + (0,))
                    dve.tensor_tensor(att[0:n, u, :], prod[0:n, 0].rearrange("p g j d -> p (g j d)"),
                                      prod[0:n, 1].rearrange("p g j d -> p (g j d)"), ALU.add).then_inc(s_att, 1)
                    dve.wait_ge(s_att, i + 1)
                elif kind == "proj":
                    job_done(dve, s + (0,))
                    dve.tensor_tensor(h_all[0:n, i, :], bank(s + (0,))[0:n, 0:D], h_all[0:n, i, :], ALU.add).then_inc(s_dr["D"], 1)
                    drained(dve, s + (0,))
                    moments(i)
                elif kind == "rstd":
                    b = s[1]
                    dve.wait_ge(s_chain, steps[0])
                    dve.tensor_scalar(ve[:, b * TT:(b + 1) * TT], mv[:, b * TT:(b + 1) * TT, 1], EPS, None, ALU.add).then_inc(s_var, 1)
                    refine(b * TT, (b + 1) * TT, b + 2)
                elif kind == "ln2":
                    normalise(i).then_inc(s_ln2, 1)
                elif kind == "router":
                    job_done(dve, s + (0,))
                    dve.tensor_copy(logit[0:n, i, :], bank(s + (0,))[0:n, 0:NE]).then_inc(s_dr["D"], 1)

            drained(dve, ("router", NT - 1, 0))
            wide = lambda x: x.rearrange("p (i o) -> p i o", o=1).to_broadcast([P, NT, NE])
            pref = cst[:, C_PREF:C_PREF + NE].rearrange("p (o e) -> p o e", o=1).to_broadcast([P, NT, NE])
            work = logit
            for c in range(2):
                m = m12[:, c, :]
                link(dve.tensor_reduce(m, work[:], AX, ALU.max))
                link(dve.tensor_tensor(w8[:], work[:], wide(m), ALU.is_equal))
                link(dve.tensor_tensor(w8[:], w8[:], pref, ALU.mult))
                link(dve.tensor_reduce(dd[:], w8[:], AX, ALU.max))
                link(dve.tensor_tensor(oh[:, c], w8[:], wide(dd[:]), ALU.is_equal))
                if c == 0:
                    link(dve.tensor_scalar(w8b[:], oh[:, 0], -3.0e38, None, ALU.mult))
                    link(dve.tensor_tensor(posn[:], logit[:], w8b[:], ALU.add))
                    work = posn
            valid = cst[:, C_VALID:C_VALID + NT]
            for c in range(2):
                link(dve.tensor_tensor(oh[:, c], oh[:, c], wide(valid), ALU.mult))
            dve.tensor_tensor(both[:], oh[:, 0], oh[:, 1], ALU.add).then_inc(s_hot, 1)
            dve.tensor_tensor(w8[:], logit[:], wide(m12[:, 0, :]), ALU.subtract).then_inc(s_shift, 1)
            dve.tensor_tensor(dd[:], m12[:, 1, :], m12[:, 0, :], ALU.subtract).then_inc(s_shift, 1)
            job_done(dve, ("rank", 0))
            job_done(dve, ("rank", 1))
            rank = bank(("rank", 0))[:, 0:NT * NE].rearrange("p (i e) -> p i e", e=NE)
            total = bank(("rank", 1))[:, 0:NT * NE].rearrange("p (i e) -> p i e", e=NE)
            link(dve.memset(pre[:, :, 0:1, :], 0.0))
            link(dve.tensor_copy(pre[:, 0, 1:NT + 1, :], total))
            cur, step = 0, 1
            while step < NT:
                dve.tensor_copy(pre[:, 1 - cur, 1:1 + step, :], pre[:, cur, 1:1 + step, :]).then_inc(s_chain, 1)
                steps[0] += 1
                link(dve.tensor_tensor(pre[:, 1 - cur, 1 + step:NT + 1, :], pre[:, cur, 1 + step:NT + 1, :],
                                       pre[:, cur, 1:NT + 1 - step, :], ALU.add))
                cur, step = 1 - cur, 2 * step
            count = pre[:, cur, NT:NT + 1, :].rearrange("p o e -> p e o").to_broadcast([P, NE, EXP_TILES])
            kk = cst[:, C_K:C_K + EXP_TILES].rearrange("p (o k) -> p o k", o=1).to_broadcast([P, NE, EXP_TILES])
            link(dve.tensor_tensor(cmp[:], count, kk, ALU.is_gt))
            link(dve.tensor_reduce(nt_e[:], cmp[:], AX, ALU.add))
            link(dve.tensor_copy(end[:, 0, :], nt_e[:]))
            u, step = 0, 1
            while step < NE:
                dve.tensor_copy(end[:, 1 - u, 0:step], end[:, u, 0:step]).then_inc(s_chain, 1)
                steps[0] += 1
                link(dve.tensor_tensor(end[:, 1 - u, step:NE], end[:, u, step:NE], end[:, u, 0:NE - step], ALU.add))
                u, step = 1 - u, 2 * step
            link(dve.tensor_tensor(base[:], end[:, u, :], nt_e[:], ALU.subtract))
            link(dve.tensor_scalar(base[:], base[:], float(P), None, ALU.mult))
            link(dve.tensor_tensor(posn[:], rank, pre[:, cur, 0:NT, :], ALU.add))
            link(dve.tensor_tensor(posn[:], posn[:], base[:].rearrange("p (o e) -> p o e", o=1).to_broadcast([P, NT, NE]), ALU.add))
            for c in range(2):
                link(dve.tensor_tensor(both[:], oh[:, c], posn[:], ALU.mult))
                link(dve.tensor_reduce(slotf[:, c, :], both[:], AX, ALU.add))
            link(dve.tensor_copy(slot[:], slotf[:]))
            tau = cst[:, C_TAU:C_TAU + SLOT_TILES].rearrange("p (t o) -> p t o", o=1).to_broadcast([P, SLOT_TILES, NE])
            ends = end[:, u, :].rearrange("p (o e) -> p o e", o=1).to_broadcast([P, SLOT_TILES, NE])
            link(dve.tensor_tensor(tcmp[:], tau, ends, ALU.is_ge))
            link(dve.tensor_reduce(texf[:], tcmp[:], AX, ALU.add))
            link(dve.tensor_scalar(texf[:], texf[:], float(NE - 1), None, ALU.min))
            link(dve.tensor_copy(tex[:], texf[:]))
            dve.sem_inc(s_dr["D"], 2)
            link(dve.tensor_scalar(within_i[:], slot[:], P - 1, None, ALU.bitwise_and))
            link(dve.tensor_scalar(tile_i[:], slot[:], P.bit_length() - 1, None, ALU.logical_shift_right))
            link(dve.tensor_copy(within[:], within_i[:]))
            link(dve.tensor_copy(tile[:], tile_i[:]))
            dve.wait_ge(s_p, 2)
            link(dve.tensor_reduce(gsum[:], w8b[:], AX, ALU.add))
            link(dve.reciprocal(gw[:, 0, :], gsum[:]))
            link(dve.tensor_tensor(gw[:, 1, :], gw[:, 1, :], gw[:, 0, :], ALU.mult))
            for c in range(2):
                weight = weights[:, c].rearrange("p i w -> p w i")
                link(dve.tensor_tensor(gw[:, c, :], gw[:, c, :], valid, ALU.mult))
                dve.tensor_copy(weight[:, 0, :], cst[:, C_ROW:C_ROW + NT])
                link(dve.tensor_copy(weight[:, 1, :], gw[:, c, :]))
                link(dve.tensor_tensor(weight[:, 2, :], gw[:, c, :], weight[:, 1, :], ALU.subtract))
            dve.wait_ge(s_hst, 16 * (NT + 1))
            dve.wait_ge(s_xst, 16 * (2 * NT + 1))
            for q in range(2 * NT // HOTS):
                c, i = divmod(q * HOTS, NT)
                if q >= 2:
                    dve.wait_ge(s_list, q - 1)
                column = lambda x, n: x[:, c, i:i + HOTS].rearrange("p (j o) -> p j o", o=1).to_broadcast([P, HOTS, n])
                col = cst[:, C_COL:C_COL + P].rearrange("p (o s) -> p o s", o=1).to_broadcast([P, HOTS, P])
                dve.tensor_tensor(hot[:, q % 2], col, column(within, P), ALU.is_equal)
                taus = cst[:, C_TAU:C_TAU + SLOT_TILES].rearrange("p (o t) -> p o t", o=1).to_broadcast([P, HOTS, SLOT_TILES])
                link(dve.tensor_tensor(at[:], taus, column(tile, SLOT_TILES), ALU.is_equal))
                x = at[:].rearrange("p j (o t) -> p j o t", o=1).to_broadcast([P, HOTS, 3, SLOT_TILES])
                y = weights[:, c, i:i + HOTS].rearrange("p j (w o) -> p j w o", o=1).to_broadcast([P, HOTS, 3, SLOT_TILES])
                link(dve.tensor_tensor(sel[:, q % 2], x, y, ALU.mult))
                dve.sem_inc(s_onehot, 1)
            dve.wait_ge(s_list, 2 * NT // HOTS)
            link(dve.tensor_copy(gate_of[:], psO[:, 2 * SLOT_TILES:3 * SLOT_TILES]))
            link(dve.tensor_tensor(gate_of[:], psO[:, SLOT_TILES:2 * SLOT_TILES], gate_of[:], ALU.add))
            link(dve.tensor_scalar(row1[:], psO[:, 0:SLOT_TILES], 0.0, cst[:, C_EMPTY:C_EMPTY + 1], ALU.is_equal, ALU.mult))
            link(dve.scalar_tensor_tensor(out=rowf[:], in0=psO[:, 0:SLOT_TILES], scalar=-1.0, in1=row1[:], op0=ALU.add, op1=ALU.add))
            link(dve.tensor_copy(row[:], rowf[:]))
            dve.sem_inc(s_route, 1)

            def slot_T(i, cur):
                dve.wait_ge(s_mx, i + 1)
                dve.wait_ge(s_h, i - 1) if not isinstance(i, int) or i >= 2 else None
                dve.tensor_copy(xh[:, cur, :], ring[0][:, 0:2 * P]).then_inc(s_xh, 1)
                dve.wait_ge(s_xh, i + 1)
                dve.tensor_tensor(xl[:, cur, :], ring[0][:, 0:2 * P], xh[:, cur, :], ALU.subtract).then_inc(s_mxT, 1)

            def low(i, cur):
                for half in range(2):
                    cols = slice(half * W, (half + 1) * W)
                    dve.wait_ge(s_hThi, 2 * i + 1 + half)
                    dve.tensor_tensor(hTl[:, cur, cols], ring[1 + half][:, 0:W], hTh[:, cur, cols],
                                      ALU.subtract).then_inc(s_hT, 1)

            def total(i, cur):
                dve.wait_ge(s_y, i + 1)
                dve.wait_ge(s_ysb, i - 1) if not isinstance(i, int) or i >= 2 else None
                dve.tensor_copy(ysum[:, cur, :], psO[:, D:2 * D]).then_inc(s_half, 1)
                dve.wait_ge(s_half, i + 1)
                dve.tensor_tensor(ysum[:, cur, :], psO[:, 0:D], ysum[:, cur, :], ALU.add).then_inc(s_ysum, 1)

            slot_T(0, 0)
            slot_T(1, 1)
            for i in range(2):
                low(i, i)
                slot_T(i + 2, i)
                total(i, i)
            with dve.Fori(1, SLOT_TILES // 2 - 1) as pair:
                for u in range(2):
                    i = 2 * pair + u
                    low(i, u)
                    slot_T(i + 2, u)
                    total(i, u)
            for i in range(SLOT_TILES - 2, SLOT_TILES):
                low(i, i % 2)
                total(i, i % 2)


def kernel(x, txt, L0_tok_W, L0_tok_b, L0_tok_class_token, L0_tok_pos_embedding, L0_attn_w_qkv, L0_attn_b_qkv,
           L0_attn_w_out, L0_attn_b_out, L0_attn_w_mem, L0_attn_b_mem, L0_attn_memory, L0_ffn_router_w,
           L0_ffn_w1, L0_ffn_w2):
    import numpy as np
    import concourse.bacc as bacc
    from concourse.bass_utils import run_bass_kernel_spmd

    f = lambda v: np.asarray(v)
    s = 16
    n = 96 // s
    x = f(x)
    pt = x.reshape(B, 3, n, s, n, s).transpose(0, 1, 2, 4, 3, 5).reshape(B, NPATCH, PD).transpose(2, 0, 1)
    patchT = np.zeros((PC, P, B, NIMG), x.dtype)
    patchT[:, :, :, 1:] = pt.reshape(PC, P, B, NPATCH)
    with_row = lambda w, row: np.concatenate([w, row.reshape(1, -1)], 0)
    cst = np.zeros((P, C_N), np.float32)
    cst[:, C_ID:C_ID + P] = np.eye(P)
    cst[:, C_TRI:C_TRI + P] = np.triu(np.ones((P, P)), 1)
    cst[:, C_ONE:C_ONE + P] = 1
    cst[:, C_PREF:C_PREF + NE] = NE - np.arange(NE)
    cst[:, C_TAU:C_TAU + SLOT_TILES] = np.arange(SLOT_TILES)
    cst[:, C_K:C_K + EXP_TILES] = P * np.arange(EXP_TILES)
    for i in range(NT):
        cst[0:rows_of(i % TT), C_VALID + i] = 1
    cst[0, C_SEL] = 1
    cst[1, C_SEL + 1:C_SEL + NIMG] = 1
    for i in range(NT):
        b, t = divmod(i, TT)
        r = np.arange(rows_of(t))
        cst[r, C_ROW + i] = b * T + (NIMG + t * P if t < TT - 1 else 0) + r + 1
    cst[:, C_EMPTY] = B * T + np.arange(P) + 1
    cst[:, C_COL:C_COL + P] = np.arange(P)
    mem = f(L0_attn_memory)[0]
    arrays = {
        "cst": cst,
        "patchT": patchT.transpose(1, 0, 2, 3),
        "tokw": f(L0_tok_W).T.reshape(PC, P, D).transpose(1, 0, 2),
        "clsb": np.concatenate([f(L0_tok_class_token), f(L0_tok_b).reshape(1, -1)], 0),
        "pos": f(L0_tok_pos_embedding),
        "txt": f(txt),
        "wqkv": with_row(f(L0_attn_w_qkv), f(L0_attn_b_qkv)),
        "wout": with_row(f(L0_attn_w_out), f(L0_attn_b_out)),
        "wmem": with_row(f(L0_attn_w_mem), f(L0_attn_b_mem)),
        "memT": with_row(mem.T, np.ones(MEM, mem.dtype)),
        "wr": f(L0_ffn_router_w).T,
        "w1": f(L0_ffn_w1).transpose(1, 0, 2).reshape(D, NE * DFF),
        "w2": f(L0_ffn_w2).reshape(NE, FC, P, D).transpose(2, 0, 1, 3).reshape(P, NE * FC * D),
    }
    nc = bacc.Bacc("TRN2", target_bir_lowering=False, num_devices=1)
    ins, aps = {}, {}
    for name, v in arrays.items():
        v = np.ascontiguousarray(v)
        ins["in_" + name] = v
        aps[name] = nc.dram_tensor("in_" + name, v.shape, mybir.dt.from_np(v.dtype), kind="ExternalInput").ap()
    out = nc.dram_tensor("out", (NROWS, D), F32, kind="ExternalOutput").ap()
    build(nc, aps, out)
    r = run_bass_kernel_spmd(nc, [ins], core_ids=[0])
    return r.results[0]["out"][0:B * T].reshape(B, T, D)
```

```python
from contextlib import ExitStack

import concourse.bass as bass
from concourse import mybir
from concourse.alu_op_type import AluOpType as ALU

F32 = mybir.dt.float32
BF16 = mybir.dt.bfloat16
U32 = mybir.dt.uint32
I32 = mybir.dt.int32
F32R = mybir.dt.float32r
ACT = mybir.ActivationFunctionType
AX = mybir.AxisListType.X

P = 128
B = 4
D = 192
DL = D - P
H, HD = 12, 16
NPATCH = 36
NIMG = NPATCH + 1
NTXT = 512
T = NIMG + NTXT
TT = 5
NT = B * TT
PD = 768
PC = PD // P
MEM = 64
GH = 4
G = H // GH
KQ = 6 * HD
KM = KQ + 4
KEYS = 5 * P
SIDE = 64
MROW = 32
QC = 183
NC = T // QC
VW = 32
NE, DFF, TOPK = 8, 768, 2
FC = DFF // P
SLOT_TILES = (B * T * TOPK + NE * (P - 1)) // P
EXP_TILES = (B * T + P - 1) // P
EPS = 1e-5
NROWS = B * T + P
HOTS = 10
SW = 1536
Q_PARTS, K_PARTS = (0, 0, 0, 1, 1, 2), (0, 1, 2, 0, 1, 0)
QKC = 2 * D // P
CHUNKS_OF = ((0, 2), (2, 3))
R = 3

C_ID, C_TRI, C_ONE = 0, P, 2 * P
C_PREF = 3 * P
C_TAU = C_PREF + NE
C_K = C_TAU + SLOT_TILES
C_VALID = C_K + EXP_TILES
C_SEL = C_VALID + NT
C_ROW = C_SEL + NIMG
C_EMPTY = C_ROW + NT
C_COL = C_EMPTY + 1
C_N = C_COL + P


def rows_of(t):
    return P if t < TT - 1 else NIMG


def weight_chunks():
    cuts = lambda n: [(c, min(SW, n - c)) for c in range(0, n, SW)]
    return [(w, c, n) for w, total in (("w1a", NE * DFF), ("w1b", NE * DFF), ("w2", NE * FC * D))
            for c, n in cuts(total)]


CHUNKS = weight_chunks()
EARLY = 4


LEAD = 8
PHASE = 0.42
WORK = {"xT": 0.3, "qk": 1.3, "v": 0.7, "split": 0.75, "stack": 0.5, "max": 0.8, "norm": 0.8, "attT": 0.3, "proj": 1.4,
        "rstd": 2.0, "ln2": 0.3, "ln2T": 0.3, "router": 0.4, "whi": 2.0, "wload": 0.5}


def plan():
    front = lambda b: [("ln1", b * TT), ("ln1", b * TT + 1), ("xT", b * TT)] + [s for t in range(TT + 1) for s in (
        ([("ln1", b * TT + t + 2)] if t + 2 < TT else []) +
        ([("xT", b * TT + t + 1)] if t + 1 < TT else []) +
        ([("qk", b * TT + t), ("v", b * TT + t)] + [("split", b * TT + t, x) for x in range(2)] if t < TT else []) +
        ([("stack", b * TT + t - 1, x) for x in range(2)] if 1 <= t else []))] + [("swap", b)]
    maxima = lambda g: [("max", g, t, j) for t in range(TT) for j in range(GH + 1 if t < TT - 1 else 3)] + [("negmax", g)]
    merge = lambda b: [s for t in range(TT + 2) for s in (
        ([("norm", b * TT + t, l) for l in range(2)] if t < TT else []) +
        ([("attT", b * TT + t - 1)] if 1 <= t <= TT else []) +
        ([("proj", b * TT + t - 2)] if 2 <= t else []))]
    gate = lambda b: [("rstd", b)] + [s for t in range(TT + 2) for s in (
        ([("ln2", b * TT + t)] if t < TT else []) +
        ([("ln2T", b * TT + t - 1)] if 1 <= t <= TT else []) +
        ([("router", b * TT + t - 2)] if 2 <= t else []))]
    units, NG = TT * NC, B * G
    fill = []

    def spread(stages, start, end):
        cost = [WORK.get(s[0], 0.1) for s in stages]
        done = 0.0
        for s, c in zip(stages, cost):
            fill.append((start + (end - start) * (done + c / 2) / sum(cost), len(fill), s))
            done += c

    for g in range(1, NG):
        spread(maxima(g), units * (g - 2 + PHASE), units * (g - 1 + PHASE))
        fill.append((units * (g - 1 + PHASE) + 3.5, len(fill), ("maxT", g)))
    for b in range(B):
        at = b * G * units
        if b + 1 < B:
            spread(front(b + 1), at, at + units * (1 + PHASE) - LEAD)
        if b > 0:
            spread(merge(b - 1) + gate(b - 1), at + (units * (1 + PHASE) - LEAD if b + 1 < B else 0), at + G * units)
    w = list(range(EARLY))
    early = [("wload", k) for k in w[:2]]
    for k in w:
        early += [("whi", k)] + ([("wload", k + 2)] if k + 2 in w else [])
    early += [("wload", EARLY), ("wload", EARLY + 1)]
    spread(early, (NG - G) * units + 1, NG * units)
    fill.sort()
    order = front(0) + [s for b in range(1, B) for s in [("img", b)] + [("moments", b * TT + t) for t in range(TT)]]
    order += [("first", 1)] + maxima(0)
    order += [("maxT", 0)]
    for n in range(NG * units):
        if n % units == 0:
            if n == 0:
                order += [s for x, _, s in fill if x < 0]
            order.append(("score", n))
        if (n + 1) % units:
            order.append(("score", n + 1))
        order += [s for x, _, s in fill if n <= x < n + 1]
        order.append(("value", n))
        if n % TT == TT - 1:
            order.append(("keep", n // TT))
    late = [[("whi", k)] + ([("wload", k + 2)] if k + 2 < len(CHUNKS) else []) for k in range(EARLY, len(CHUNKS))]
    order += sum(late[0:2], []) + merge(B - 1) + sum(late[2:4], []) + gate(B - 1)
    order += sum(late[4:5], []) + [("gates",)] + sum(late[5:], [])
    return order


ORDER = plan()
JOBS = {"img": "D", "mem": "AA", "memT": "AA", "xT": "A", "qk": "A", "v": "A", "stack": "A", "max": "D",
        "maxT": "A", "norm": "D", "attT": "A", "proj": "D", "ln2T": "A", "router": "D", "rank": "DD"}


def ring_plan():
    place, drains, count = {}, [], {"A": 0, "D": 0}
    for s in [("mem",), ("img", 0), ("memT",)] + ORDER + [("rank",)]:
        for part, who in enumerate(JOBS.get(s[0], "")):
            count[who] += 1
            place[s + (part,)] = len(drains)
            drains.append((who, count[who]))
    return place, drains


PLACE, DRAINS = ring_plan()


def build(nc, a, out):
    ctx = ExitStack()
    sb = lambda name, shape, dt=F32: ctx.enter_context(nc.sbuf_tensor(name, shape, dt))
    sem = lambda name: ctx.enter_context(nc.semaphore(name))
    with ctx:
        cst = sb("cst", [P, C_N])
        ident, tri, ones = cst[:, C_ID:C_ID + P], cst[:, C_TRI:C_TRI + P], cst[:, C_ONE:C_ONE + P]
        identb = sb("identb", [P, P], BF16)
        top = lambda name, shape, dt=F32: nc.sbuf_tensor(name, shape, dt, side="right")
        with top("rows", [P, 2, NT, D]) as rows:
            h_all, xn = rows[:, 0], rows[:, 1]
        with top("hot", [P, 2, HOTS, P], F32R) as hot, top("sel", [P, 2, HOTS, 3, SLOT_TILES], F32R) as sel:
            pass
        mx_in = ctx.enter_context(top("mx_in", [P, 2, 2 * P]))
        xh = ctx.enter_context(top("xh", [P, 2, 2 * P], F32R))
        xl = ctx.enter_context(top("xl", [P, 2, 2 * P], F32R))
        yb = ctx.enter_context(top("yb", [P, 2, D]))
        hg = ctx.enter_context(top("hg", [P, 2, DFF]))
        hTh = ctx.enter_context(top("hTh", [P, 2, DFF], F32R))
        hTl = ctx.enter_context(top("hTl", [P, 2, DFF], F32R))
        ysum = ctx.enter_context(top("ysum", [P, 2, D]))
        last_rows = 2 * (2 * D + 6 * P + 3 * DFF)
        ctx.enter_context(top("rows_rest", [P, 2 * NT * D - last_rows]))
        wout = [sb("wout_a", [P, D]), sb("wout_b", [DL + 1, D])]
        wr = [sb("wr_a", [P, NE]), sb("wr_b", [DL, NE])]
        stats = sb("stats", [P, NT, 6])
        mv = sb("mv", [P, NT, 2])
        ve = sb("ve", [P, NT])
        lnv = sb("lnv", [P, NT])
        r0 = sb("r0", [P, NT])
        rn = sb("rn", [P, NT])
        rstd = sb("rstd", [P, NT])
        xT = [sb("xT_a", [P, 2, P]), sb("xT_b", [DL + 1, 2, P])]
        logit = sb("logit", [P, NT, NE])
        koffb = sb("koffb", [KM - KQ, KEYS], BF16)
        with ExitStack() as first:
            fsb = lambda name, shape: first.enter_context(nc.sbuf_tensor(name, shape, F32))
            patchT = fsb("patchT", [P, PC, B, NIMG])
            tokw = fsb("tokw", [P, PC, D])
            clsb = fsb("clsb", [2, D])
            pos = fsb("pos", [NIMG, D])
            wmem = [fsb("wmem_a", [P, D]), fsb("wmem_b", [DL + 1, D])]
            memT = [fsb("memT_a", [P, MEM]), fsb("memT_b", [DL + 1, MEM])]
            koff = fsb("koff", [KM - KQ, KEYS])
            wqkv = [fsb("wqkv_a", [P, 3 * D]), fsb("wqkv_b", [DL + 1, 3 * D])]
        oh = sb("oh", [P, 2, NT, NE])
        w8 = sb("w8", [P, NT, NE])
        w8b = sb("w8b", [P, NT, NE])
        posn = sb("posn", [P, NT, NE])
        both = sb("both", [P, NT, NE])
        m12 = sb("m12", [P, 2, NT])
        dd = sb("dd", [P, NT])
        gsum = sb("gsum", [P, NT])
        gw = sb("gw", [P, 2, NT])
        pre = sb("pre", [P, 2, NT + 1, NE])
        cmp = sb("cmp", [P, NE, EXP_TILES])
        nt_e = sb("nt_e", [P, NE])
        end = sb("end", [P, 2, NE])
        base = sb("base", [P, NE])
        slotf = sb("slotf", [P, 2, NT])
        slot = sb("slot", [P, 2, NT], I32)
        within_i = sb("within_i", [P, 2, NT], I32)
        tile_i = sb("tile_i", [P, 2, NT], I32)
        within = sb("within", [P, 2, NT])
        tile = sb("tile", [P, 2, NT])
        weights = sb("weights", [P, 2, NT, 3], F32R)
        at = sb("at", [P, HOTS, SLOT_TILES])
        tcmp = sb("tcmp", [P, SLOT_TILES, NE])
        texf = sb("texf", [P, SLOT_TILES])
        tex = sb("tex", [P, SLOT_TILES], I32)
        row1 = sb("row1", [P, SLOT_TILES])
        rowf = sb("rowf", [P, SLOT_TILES])
        row = sb("row", [P, SLOT_TILES], U32)
        gate_of = sb("gate_of", [P, SLOT_TILES])
        stage = sb("stage", [P, 2, SW])

        with ExitStack() as attention:
            asb = lambda name, shape, dt=F32: attention.enter_context(nc.sbuf_tensor(name, shape, dt))
            qst, kst, val = [], [], []
            for sl in range(2):
                qst.append(asb(f"qst{sl}", [P, H, T], BF16))
                kst.append(asb(f"kst{sl}", [P, H, KEYS], BF16))
                val.append(asb(f"val{sl}", [P, 6, H, VW]))
                if sl == 0:
                    qk = asb("qk", [P, 2, 2 * D])
                    qkp = asb("qk_parts", [P, 2, 3, 2 * D], BF16)
                    rest = asb("rest", [P, 2 * D])
                    partsT = asb("partsT", [P, QKC, 3, KEYS], BF16)
            mx = asb("mx", [P, 2, TT, GH])
            mt = asb("mt", [P, 2, TT, GH, 2])
            mp = asb("mp", [P, 2, TT, GH, 4], BF16)
            mrow = asb("mrow", [MROW + 8, T], BF16)
            pr = asb("pr", [P, 3, 2, 2 * QC])
            oT = asb("oT", [P, 2, G, 2, T])
            rec = asb("rec", [P, 2, G, GH])
            prod = asb("prod", [P, 2, G, GH, HD])
            att = asb("att", [P, 2, D])
        w1a = [sb("w1a_high", [P, NE * DFF], F32R), sb("w1a_low", [P, NE * DFF], F32R)]
        w1b = sb("w1b", [P, NE * DFF], F32R)
        w2 = sb("w2", [P, NE * FC, 2, D], F32R)

        psS = ctx.enter_context(nc.psum_tensor("psS", [P, 2, 2, 512], F32))
        psO = ctx.enter_context(nc.psum_tensor("psO", [P, 512], F32))
        rings = ctx.enter_context(nc.psum_tensor("rings", [P, R, 512], F32))
        ring = [rings[:, i, :] for i in range(R)]

        swap = nc.dram_tensor("parts_transposed", (B, 2 * D, 3, KEYS), BF16, kind="Internal").ap()
        xrow = nc.dram_tensor("normalised", (NROWS, 2 * P), F32, kind="Internal").ap()

        ld_cst, ld_img, ld_first, ld_txt, ld_qkv, ld_mem, ld_out = (sem(n) for n in (
            "ld_cst", "ld_img", "ld_first_txt", "ld_txt", "ld_qkv", "ld_mem", "ld_out"))
        ld_w = [sem("ld_weights_even"), sem("ld_weights_odd")]
        s_whi, s_wlo = sem("s_weights_high"), sem("s_weights_low")
        s_hst, s_xst = sem("s_residual_stored"), sem("s_normalised_stored")
        s_ring = sem("s_ring")
        s_dr = {"A": sem("s_drain_act"), "D": sem("s_drain_dve")}
        s_chain = sem("s_chain")
        s_achain = sem("s_achain")
        s_const = sem("s_const")
        s_var, s_r0 = sem("s_var"), sem("s_r0")
        s_xn = sem("s_xn")
        s_split = sem("s_split")
        s_memsplit = sem("s_memsplit")
        s_koff, s_koffst = sem("s_koff"), sem("s_koff_placed")
        s_swap = sem("s_swap_stored")
        s_load = [sem(f"s_stacked_group{j}") for j in range(G)]
        s_neg = sem("s_neg")
        s_mrow = sem("s_mrow")
        s_moff = sem("s_moff")
        s_score, s_exp, s_value, s_keep = sem("s_score"), sem("s_exp"), sem("s_value"), sem("s_keep")
        s_att = sem("s_att")
        s_ln2 = sem("s_ln2")
        s_shift, s_p = sem("s_shift"), sem("s_p")
        s_hot = sem("s_hot")
        s_onehot = sem("s_onehot")
        s_list = sem("s_list")
        s_route = sem("s_route")
        s_half = sem("s_y_half")
        s_xh = sem("s_slot_xT_high")
        s_x = [sem("s_slot_x_even"), sem("s_slot_x_odd")]
        s_mx, s_mxT = sem("s_slot_xT_ps"), sem("s_slot_xT")
        s_h, s_g, s_hTp = sem("s_hidden"), sem("s_gelu"), sem("s_hiddenT_ps")
        s_hThi, s_hT = sem("s_hiddenT_high"), sem("s_hiddenT")
        s_y, s_ysum, s_ysb = sem("s_y"), sem("s_y_sum"), sem("s_y_sbuf")
        s_acc = sem("s_accumulated")

        W = DFF // 2
        N_CONST = 14

        def bank(key):
            return ring[PLACE[key] % R]

        def job_free(eng, key):
            k = PLACE[key] - R
            if k >= 0:
                who, n = DRAINS[k]
                eng.wait_ge(s_dr[who], n)

        def job_done(eng, key):
            eng.wait_ge(s_ring, PLACE[key] + 1)

        def drained(eng, key):
            who, n = DRAINS[PLACE[key]]
            eng.wait_ge(s_dr[who], n)

        block = ctx.enter_context(nc.Block())

        @block.sync
        def _(sp):
            sp.dma_start(cst[:], a["cst"]).then_inc(ld_cst, 16)

            def load(dst, src, done):
                sp.dma_start(dst[0][:], a[src][0:P, :]).then_inc(done, 16)
                sp.dma_start(dst[1][:], a[src][P:P + dst[1].shape[0], :]).then_inc(done, 16)

            def load_text(b, done):
                sp.dma_start(h_all[:, b * TT:b * TT + TT - 1, :],
                             a["txt"][b].rearrange("(t p) d -> p t d", p=P)).then_inc(done, 16)

            sp.dma_start(koff[:], a["koff"]).then_inc(ld_mem, 16)
            load(memT, "memT", ld_mem)
            load(wmem, "wmem", ld_mem)
            load_text(0, ld_first)
            load(wqkv, "wqkv", ld_qkv)
            for b in range(1, B):
                load_text(b, ld_txt)
            load(wout, "wout", ld_out)
            load(wr, "wr", ld_out)
            sp.wait_ge(ld_cst, 16)
            for dst, width, done in ((out, D, s_hst), (xrow, 2 * P, s_xst)):
                sp.dma_start(dst[B * T:NROWS, :], cst[:, 0:width]).then_inc(done, 16)
            sp.wait_ge(s_koff, 1)
            for sl in range(2):
                sp.dma_start(kst[sl][KQ:KM, :, :],
                             koffb[:].rearrange("p (o k) -> p o k", o=1).to_broadcast([KM - KQ, H, KEYS])).then_inc(s_koffst, 16)
            for s in ORDER:
                if s[0] == "swap":
                    b = s[1]
                    drained(sp, ("stack", b * TT + TT - 1, 1, 0))
                    sp.dma_start(swap[b].rearrange("(c p) s t -> p c s t", p=P), partsT[:]).then_inc(s_swap, 16)
                    sp.wait_ge(s_swap, 16 * (b + 1))
                    if b >= 2:
                        sp.wait_ge(s_score, (b - 1) * G * NC * TT)
                    for j in range(G):
                        if b >= 1:
                            sp.wait_ge(s_load[j], 16 * 2 * 6 * b)
                        for dst, row0, cols, which in ((qst, 0, T, Q_PARTS), (kst, D, KEYS, K_PARTS)):
                            heads = slice(j * GH, (j + 1) * GH)
                            src = swap[b, row0:row0 + D].rearrange("(h d) s t -> d h s t", d=HD)
                            for k, part in enumerate(which):
                                sp.dma_start(dst[b % 2][k * HD:(k + 1) * HD, heads, :],
                                             src[:, heads, part, 0:cols]).then_inc(s_load[j], 16)
                elif s[0] == "maxT":
                    g = s[1]
                    sp.wait_ge(s_mrow, g + 1)
                    for j in range(GH):
                        sp.dma_start(qst[g // G % 2][KQ:KM, (g % G) * GH + j, :],
                                     mrow[MROW * (j // 2) + 4 * (j % 2):MROW * (j // 2) + 4 * (j % 2) + 4, :]).then_inc(s_moff, 16)
                elif s[0] == "ln2":
                    i = s[1]
                    b, t = divmod(i, TT)
                    n = rows_of(t)
                    r = b * T + (NIMG + t * P if t < TT - 1 else 0)
                    sp.wait_ge(s_ln2, i + 1)
                    sp.dma_start(out[r:r + n, :], h_all[0:n, i, :]).then_inc(s_hst, 16)
                    sp.dma_start(xrow[r:r + n, 0:D], xn[0:n, i, :]).then_inc(s_xst, 16)
                    sp.dma_start(xrow[r:r + n, D:2 * P], xn[0:n, i, P:D]).then_inc(s_xst, 16)
                elif s[0] == "wload":
                    k = s[1]
                    w, c, n = CHUNKS[k]
                    if k >= 2:
                        sp.wait_ge(s_wlo, k - 1)
                    if w == "w1b":
                        for half in range(2):
                            sp.dma_start(stage[half * DL:(half + 1) * DL, k % 2, 0:n],
                                         a["w1"][P:D, c:c + n]).then_inc(ld_w[k % 2], 16)
                    else:
                        src = a["w1"][0:P, c:c + n] if w == "w1a" else a["w2"][:, c:c + n]
                        sp.dma_start(stage[:, k % 2, 0:n], src).then_inc(ld_w[k % 2], 16)

        @block.gpsimd
        def _(pool):
            fills = [f for v in val for f in (
                (v[:], 0.0), (v[:, 0:TT - 1, :, HD:HD + 1], 1.0),
                (v[0:NIMG, TT - 1:TT, :, HD:HD + 1], 1.0), (v[MEM:P, TT:TT + 1, :, HD:HD + 1], 1.0))] + [
                     (xT[1][DL:DL + 1, :, :], 1.0), (qk[0:MEM, 0, 0:D], 0.0), (mv[:], 1.0), (mx[:], 0.0),
                     (mt[:], 0.0), (logit[:], 0.0)]
            for k, (dst, v) in enumerate(fills):
                pool.memset(dst, v).then_inc(s_const, 1)
                pool.wait_ge(s_const, k + 1)
            for s in ORDER:
                if s[0] == "whi":
                    k = s[1]
                    w, c, n = CHUNKS[k]
                    pool.wait_ge(s_whi, k + 1)
                    if w == "w1b":
                        ins = pool.tensor_tensor(w1b[DL:P, c:c + n], stage[DL:P, k % 2, 0:n], w1b[DL:P, c:c + n], ALU.subtract)
                    elif w == "w1a":
                        ins = pool.tensor_tensor(w1a[1][:, c:c + n], stage[:, k % 2, 0:n], w1a[0][:, c:c + n], ALU.subtract)
                    else:
                        block = w2[:, c // D:(c + n) // D]
                        ins = pool.tensor_tensor(block[:, :, 1, :], stage[:, k % 2, 0:n].rearrange("p (x d) -> p x d", d=D),
                                                 block[:, :, 0, :], ALU.subtract)
                    ins.then_inc(s_wlo, 1)
                    pool.wait_ge(s_wlo, k + 1)

            def gather(i):
                pool.indirect_dma_start(
                    out=mx_in[:, i % 2, :], out_offset=None, in_=xrow,
                    in_offset=bass.IndirectOffsetOnAxis(ap=row[:, i:i + 1], axis=0)).then_inc(s_x[i % 2], 16)

            pool.wait_ge(s_xst, 16 * (2 * NT + 1))
            pool.wait_ge(s_route, 1)
            for i in range(4):
                if i >= 2:
                    pool.wait_ge(s_mx, i - 1)
                gather(i)
            for i in range(SLOT_TILES):
                if i + 4 < SLOT_TILES:
                    pool.wait_ge(s_mx, i + 3)
                    gather(i + 4)
                pool.wait_ge(s_ysb, i + 1)
                if i == 0:
                    pool.wait_ge(s_hst, 16 * (NT + 1))
                else:
                    pool.wait_ge(s_acc, 16 * i)
                pool.indirect_dma_start(
                    out=out, out_offset=bass.IndirectOffsetOnAxis(ap=row[:, i:i + 1], axis=0),
                    in_=yb[:, i % 2, :], in_offset=None, compute_op=ALU.add).then_inc(s_acc, 16)
            pool.wait_ge(s_acc, 16 * SLOT_TILES)

        @block.scalar
        def _(act):
            def power(n0, n1, k):
                act.wait_ge(s_var, k)
                act.activation(lnv[:, n0:n1], ve[:, n0:n1], ACT.Ln).then_inc(s_achain, 1)
                act.wait_ge(s_achain, k)
                act.activation(r0[:, n0:n1], lnv[:, n0:n1], ACT.Exp, scale=-0.5).then_inc(s_r0, 1)

            def transposed(dst, key, buf, n):
                job_done(act, key)
                act.activation(dst[0][:, buf, 0:n], bank(key)[:, 0:n], ACT.Copy)
                act.activation(dst[1][0:DL, buf, 0:n], bank(key)[0:DL, P:P + n], ACT.Copy).then_inc(s_dr["A"], 1)

            act.dma_start(tokw[:], a["tokw"]).then_inc(ld_img, 16)
            act.dma_start(patchT[:], a["patchT"]).then_inc(ld_img, 16)
            act.dma_start(clsb[:], a["clsb"]).then_inc(ld_img, 16)
            act.dma_start(pos[:], a["pos"]).then_inc(ld_img, 16)
            act.wait_ge(s_const, N_CONST)
            job_done(act, ("mem", 0))
            act.activation(qk[0:MEM, 0, D:2 * D], bank(("mem", 0))[0:MEM, 0:D], ACT.Copy).then_inc(s_dr["A"], 1)
            job_done(act, ("mem", 1))
            for sl in range(2):
                ins = act.activation(val[sl][MEM:P, TT, :, 0:HD],
                                     bank(("mem", 1))[MEM:P, 0:D].rearrange("p (h d) -> p h d", h=H), ACT.Copy)
            ins.then_inc(s_dr["A"], 1)
            act.activation(koffb[:], koff[:], ACT.Copy).then_inc(s_koff, 1)

            def transposed_parts(key, x, n, col):
                c0, c1 = CHUNKS_OF[x]
                job_done(act, key)
                src = bank(key)[:].bitcast(BF16)[:, 0:(c1 - c0) * 3 * P].rearrange("p (x t) -> p x t", t=P)
                dst = partsT[:, c0:c1].rearrange("p c s t -> p (c s) t")
                ins = act.activation(dst[:, :, col:col + n], src[:, :, 0:n], ACT.Copy)
                if n == NIMG:
                    ins = act.activation(dst[:, :, T:KEYS - MEM], src[:, :, 0:KEYS - MEM - T], ACT.Copy)
                ins.then_inc(s_dr["A"], 1)

            for x in range(2):
                transposed_parts(("memT", x), x, MEM, KEYS - MEM)
            power(0, TT, 1)

            for s in ORDER:
                kind = s[0]
                if kind == "first":
                    power(TT, NT, 2)
                elif kind in ("xT", "attT", "ln2T"):
                    i = s[1]
                    transposed(xT, s + (0,), i % 2, rows_of(i % TT))
                elif kind == "qk":
                    i = s[1]
                    n = rows_of(i % TT)
                    job_done(act, s + (0,))
                    if i >= 2:
                        act.wait_ge(s_split, 2 * (i - 2) + 1)
                    else:
                        act.wait_ge(s_memsplit, 1)
                    act.activation(qk[0:n, i % 2, :], bank(s + (0,))[0:n, 0:2 * D], ACT.Copy).then_inc(s_dr["A"], 1)
                elif kind == "v":
                    b, t = divmod(s[1], TT)
                    n = rows_of(t)
                    job_done(act, s + (0,))
                    if b >= 2:
                        act.wait_ge(s_value, (b - 1) * G * NC * TT)
                    act.activation(val[b % 2][0:n, t, :, 0:HD],
                                   bank(s + (0,))[0:n, 0:D].rearrange("p (h d) -> p h d", h=H), ACT.Copy).then_inc(s_dr["A"], 1)
                elif kind == "stack":
                    b, t = divmod(s[1], TT)
                    if b >= 1 and t == 0 and s[2] == 0:
                        act.wait_ge(s_swap, 16 * b)
                    transposed_parts(s + (0,), s[2], rows_of(t), t * P)
                elif kind == "maxT":
                    g = s[1]
                    job_done(act, s + (0,))
                    if g >= 1:
                        act.wait_ge(s_moff, 16 * GH * g)
                    for r in (0, MROW):
                        ins = act.activation(mrow[r:r + 8, :], bank(s + (0,))[:].bitcast(BF16)[r:r + 8, 0:T], ACT.Copy)
                    ins.then_inc(s_dr["A"], 1)
                    act.wait_ge(s_dr["A"], DRAINS[PLACE[s + (0,)]][1])
                    act.sem_inc(s_mrow, 1)
                elif kind == "score":
                    n = s[1]
                    act.wait_ge(s_score, n + 1)
                    if n >= 3:
                        act.wait_ge(s_value, n - 2)
                    act.activation(pr[:, n % 3], psS[:, n % 2, :, 0:2 * QC], ACT.Exp, scale=HD ** -0.5).then_inc(s_exp, 1)
                elif kind == "keep":
                    c = s[1]
                    g, q = divmod(c, NC)
                    b = g // G
                    act.wait_ge(s_value, (c + 1) * TT)
                    if b >= 2:
                        act.wait_ge(s_att, (b - 1) * TT)
                    act.activation(oT[:, b % 2, g % G, :, q * QC:(q + 1) * QC],
                                   psO[:, 0:2 * QC].rearrange("p (l q) -> p l q", l=2), ACT.Copy).then_inc(s_keep, 1)
                elif kind == "gates":
                    act.wait_ge(s_shift, 2)
                    act.activation(w8b[:], w8[:], ACT.Exp).then_inc(s_p, 1)
                    act.activation(gw[:, 1, :], dd[:], ACT.Exp).then_inc(s_p, 1)
                elif kind == "whi":
                    k = s[1]
                    w, c, n = CHUNKS[k]
                    act.wait_ge(ld_w[k % 2], 16 * sum(2 if CHUNKS[x][0] == "w1b" else 1 for x in range(k % 2, k + 1, 2)))
                    if k == 0:
                        act.wait_ge(s_value, (B - 1) * G * NC * TT)
                        act.wait_ge(s_split, 2 * NT)
                        act.wait_ge(s_swap, 16 * B)
                    elif k == EARLY:
                        act.wait_ge(s_value, B * G * NC * TT)
                    elif k == len(CHUNKS) - 2:
                        job_done(act, ("attT", NT - 1, 0))
                    if w == "w2":
                        act.activation(w2[:, c // D:(c + n) // D, 0, :],
                                       stage[:, k % 2, 0:n].rearrange("p (x d) -> p x d", d=D), ACT.Copy).then_inc(s_whi, 1)
                    else:
                        dst = w1a[0] if w == "w1a" else w1b
                        act.activation(dst[:, c:c + n], stage[:, k % 2, 0:n], ACT.Copy).then_inc(s_whi, 1)
                elif kind == "rstd":
                    power(s[1] * TT, (s[1] + 1) * TT, s[1] + 3)
            def gelu(i, cur):
                act.wait_ge(s_h, i + 1)
                act.wait_ge(s_hTp, i - 1) if not isinstance(i, int) or i >= 2 else None
                act.activation(hg[:, cur, :].rearrange("p (a f) -> p a f", a=2), psS[:, cur, :, 0:W], ACT.Gelu_apprx_tanh).then_inc(s_g, 1)

            def high(i, cur):
                act.wait_ge(s_hTp, i + 1)
                act.wait_ge(s_y, i - 1) if not isinstance(i, int) or i >= 2 else None
                for half in range(2):
                    act.activation(hTh[:, cur, half * W:(half + 1) * W], ring[1 + half][:, 0:W], ACT.Copy).then_inc(s_hThi, 1)

            def result(i, cur):
                act.wait_ge(s_ysum, i + 1)
                act.wait_ge(s_acc, 16 * i - 16) if not isinstance(i, int) or i >= 2 else None
                act.activation(yb[:, cur, :], ysum[:, cur, :], ACT.Copy, scale=gate_of[:, bass.ds(i, 1)]).then_inc(s_ysb, 1)

            def item(i, cur):
                high(i, cur)
                if not isinstance(i, int) or i >= 1:
                    result(i - 1, 1 - cur)
                if not isinstance(i, int) or i + 1 < SLOT_TILES:
                    gelu(i + 1, 1 - cur)

            gelu(0, 0)
            for i in range(4):
                item(i, i % 2)
            with act.Fori(2, SLOT_TILES // 2 - 1) as pair:
                for u in range(2):
                    item(2 * pair + u, u)
            for i in range(SLOT_TILES - 2, SLOT_TILES):
                item(i, i % 2)
            result(SLOT_TILES - 1, 1)

        @block.tensor
        def _(pe):
            def group(dst, pairs, **kw):
                for n, (l, r) in enumerate(pairs):
                    ins = pe.matmul(dst, l, r, start=(n == 0), stop=(n == len(pairs) - 1), **kw)
                return ins

            def transpose2(dst, src, n):
                pe.transpose(dst[:, 0:n], src[:, 0:P], ident[0:n, 0:n])
                return pe.transpose(dst[0:DL, P:P + n], src[:, P:D], ident[0:n, 0:n])

            pe.wait_ge(ld_cst, 16)

            def image(b):
                key = ("img", b, 0)
                job_free(pe, key)
                group(bank(key)[0:NIMG, 0:D], [(cst[0:2, C_SEL:C_SEL + NIMG], clsb[:])] +
                      [(patchT[:, k, b, :], tokw[:, k, :]) for k in range(PC)]).then_inc(s_ring, 1)

            pe.wait_ge(ld_mem, 80)
            for c, rows in enumerate((slice(0, MEM), slice(MEM, P))):
                key = ("mem", c)
                job_free(pe, key)
                group(bank(key)[rows, 0:D], [(memT[k][:], wmem[k][:]) for k in range(2)]).then_inc(s_ring, 1)
            pe.wait_ge(ld_img, 64)
            image(0)
            pe.wait_ge(s_memsplit, 1)

            def transpose_parts(key, x, buf, n):
                c0, c1 = CHUNKS_OF[x]
                job_free(pe, key)
                for c in range(c0, c1):
                    for part in range(3):
                        at_col = ((c - c0) * 3 + part) * P
                        ins = pe.transpose(bank(key)[:].bitcast(BF16)[:, at_col:at_col + n],
                                           qkp[0:n, buf, part, c * P:(c + 1) * P], identb[0:n, 0:n])
                ins.then_inc(s_ring, 1)

            for x in range(2):
                transpose_parts(("memT", x), x, 0, MEM)
            pe.wait_ge(ld_qkv, 32)
            pe.wait_ge(ld_out, 64)

            for s in ORDER:
                kind = s[0]
                if JOBS.get(kind):
                    i = s[1]
                    b, t = divmod(i, TT)
                    n = rows_of(t)
                if kind == "img":
                    image(s[1])
                elif kind == "xT":
                    pe.wait_ge(s_xn, i + 1)
                    job_free(pe, s + (0,))
                    transpose2(bank(s + (0,)), xn[0:n, i, :], n).then_inc(s_ring, 1)
                elif kind in ("qk", "v"):
                    drained(pe, ("xT", i, 0))
                    lhs = (xT[0][:, i % 2, 0:n], xT[1][:, i % 2, 0:n])
                    c0, c1 = (0, 2 * D) if kind == "qk" else (2 * D, 3 * D)
                    job_free(pe, s + (0,))
                    group(bank(s + (0,))[0:n, 0:c1 - c0],
                          [(lhs[k], wqkv[k][:, c0:c1]) for k in range(2)]).then_inc(s_ring, 1)
                elif kind == "stack":
                    pe.wait_ge(s_split, 2 * i + 2)
                    transpose_parts(s + (0,), s[2], i % 2, n)
                elif kind == "max":
                    _, g, t, j = s
                    n, sl = rows_of(t), g // G % 2
                    if t == 0 and j == 0:
                        pe.wait_ge(s_load[g % G], 16 * 2 * 6 * (g // G + 1))
                    job_free(pe, s + (0,))
                    if t < TT - 1 and j < GH:
                        products = [(j, 0, 0, 0, NTXT)]
                    elif t < TT - 1:
                        products = [(x, 0, x * P, NTXT, KEYS) for x in range(GH)]
                    elif j < 2:
                        products = [(j, 0, 0, 0, NTXT), (j + 2, SIDE, 0, 0, NTXT)]
                    else:
                        products = [(x, x // 2 * SIDE, x % 2 * P, NTXT, KEYS) for x in range(GH)]
                    for x, r, c, k0, k1 in products:
                        h = (g % G) * GH + x
                        ins = pe.matmul(bank(s + (0,))[r:r + n, c:c + k1 - k0], qst[sl][0:KQ, h, t * P:t * P + n],
                                        kst[sl][0:KQ, h, k0:k1], start=True, stop=True)
                    ins.then_inc(s_ring, 1)
                elif kind == "maxT":
                    g = s[1]
                    pe.wait_ge(s_neg, g + 1)
                    job_free(pe, s + (0,))
                    for t in range(TT):
                        n = rows_of(t)
                        for half in range(2):
                            r, j = (0, 2 * half) if t < TT - 1 else (SIDE * half, 0)
                            ins = pe.transpose(bank(s + (0,))[:].bitcast(BF16)[MROW * half:MROW * half + 8, t * P:t * P + n],
                                               mp[r:r + n, g % 2, t, j:j + 2].rearrange("p j c -> p (j c)"),
                                               identb[r:r + n, r:r + n])
                    ins.then_inc(s_ring, 1)
                elif kind == "score":
                    n = s[1]
                    c, k = divmod(n, TT)
                    g, c = divmod(c, NC)
                    sl = g // G % 2
                    if n == 0:
                        pe.wait_ge(s_koffst, 32)
                    if c == 0 and k == 0:
                        pe.wait_ge(s_moff, 16 * GH * (g + 1))
                    if n >= 2:
                        pe.wait_ge(s_exp, n - 1)
                    for j in range(GH):
                        h = (g % G) * GH + j
                        ins = pe.matmul(psS[:, n % 2, j // 2, (j % 2) * QC:(j % 2 + 1) * QC],
                                        kst[sl][0:KM, h, k * P:(k + 1) * P],
                                        qst[sl][0:KM, h, c * QC:(c + 1) * QC], start=True, stop=True)
                    ins.then_inc(s_score, 1)
                elif kind == "value":
                    n = s[1]
                    c, k = divmod(n, TT)
                    g = c // NC
                    sl = g // G % 2
                    pe.wait_ge(s_exp, n + 1)
                    if k == 0 and c >= 1:
                        pe.wait_ge(s_keep, c)
                    for j in range(GH):
                        h = (g % G) * GH + j
                        rhs = pr[:, n % 3, j // 2, (j % 2) * QC:(j % 2 + 1) * QC]
                        ins = pe.matmul(psO[32 * j:32 * j + VW, 0:QC], val[sl][:, k, h, :], rhs,
                                        start=(k == 0), stop=(k == TT - 1))
                    if k == TT - 1:
                        for j in range(GH):
                            h = (g % G) * GH + j
                            rhs = pr[:, n % 3, j // 2, (j % 2) * QC:(j % 2 + 1) * QC]
                            ins = pe.matmul(psO[32 * j:32 * j + VW, QC:2 * QC], val[sl][:, TT, h, :], rhs,
                                            start=True, stop=True)
                    ins.then_inc(s_value, 1)
                elif kind == "norm":
                    l = s[2]
                    if t == 0:
                        pe.wait_ge(s_keep, (b + 1) * G * NC)
                    job_free(pe, s + (0,))
                    for g in range(G):
                        ins = pe.transpose(bank(s + (0,))[0:n, g * P:(g + 1) * P],
                                           oT[:, b % 2, g, l, t * P:t * P + n], ident)
                    ins.then_inc(s_ring, 1)
                elif kind == "attT":
                    pe.wait_ge(s_att, i + 1)
                    job_free(pe, s + (0,))
                    transpose2(bank(s + (0,)), att[0:n, i % 2, :], n).then_inc(s_ring, 1)
                elif kind == "proj":
                    drained(pe, ("attT", i, 0))
                    job_free(pe, s + (0,))
                    group(bank(s + (0,))[0:n, 0:D], [(xT[k][:, i % 2, 0:n], wout[k][:]) for k in range(2)]).then_inc(s_ring, 1)
                elif kind == "ln2T":
                    pe.wait_ge(s_ln2, i + 1)
                    job_free(pe, s + (0,))
                    transpose2(bank(s + (0,)), xn[0:n, i, :], n).then_inc(s_ring, 1)
                elif kind == "router":
                    drained(pe, ("ln2T", i, 0))
                    job_free(pe, s + (0,))
                    group(bank(s + (0,))[0:n, 0:NE],
                          [(xT[0][:, i % 2, 0:n], wr[0][:]), (xT[1][0:DL, i % 2, 0:n], wr[1][:])]).then_inc(s_ring, 1)

            pe.wait_ge(s_hot, 1)
            for c, m in enumerate((tri, ones)):
                job_free(pe, ("rank", c))
                pe.matmul(bank(("rank", c))[:, 0:NT * NE], m, both[:].rearrange("p i e -> p (i e)"),
                          start=True, stop=True).then_inc(s_ring, 1)

            pe.wait_ge(s_keep, B * G * NC)
            for q in range(2 * NT // HOTS):
                pe.wait_ge(s_onehot, q + 1)
                for j in range(HOTS):
                    ins = pe.matmul(psO[:, 0:3 * SLOT_TILES], hot[:, q % 2, j, :], sel[:, q % 2, j].rearrange("p c t -> p (c t)"),
                                    start=(q + j == 0), stop=(q == 2 * NT // HOTS - 1 and j == HOTS - 1))
                ins.then_inc(s_list, 1)

            def load_expert(i):
                return pe.value_load(tex[0:1, bass.ds(i, 1)], min_val=0, max_val=NE - 1)

            def slot_T(i, cur, pair, down_next=False):
                pe.wait_ge(s_mxT, 1) if isinstance(i, int) and i == 1 else None
                pe.wait_ge(s_x[cur], 16 * (pair + 1))
                pe.transpose(ring[0][:, 0:P], mx_in[:, cur, 0:P], ident)
                if down_next:
                    pe.wait_ge(s_hT, 2 * i - 3)
                pe.transpose(ring[0][:, P:2 * P], mx_in[:, cur, P:2 * P], ident).then_inc(s_mx, 1)

            def up(i, cur, e):
                pe.wait_ge(s_mxT, i + 1)
                for half in range(2):
                    cols = bass.ds(e * DFF + half * W, W)
                    ins = group(psS[:, cur, half, 0:W],
                                [(xh[:, cur, 0:P], w1a[0][:, cols]), (xl[:, cur, 0:P], w1a[0][:, cols]),
                                 (xh[:, cur, 0:P], w1a[1][:, cols]),
                                 (xh[:, cur, P:2 * P], w1b[:, cols]), (xl[0:DL, cur, P:2 * P], w1b[0:DL, cols])])
                ins.then_inc(s_h, 1)

            def hidden_T(i, cur):
                pe.wait_ge(s_g, i + 1)
                for c in range(FC):
                    ins = pe.transpose(ring[1 + c // 3][:, (c % 3) * P:(c % 3 + 1) * P], hg[:, cur, c * P:(c + 1) * P], ident)
                ins.then_inc(s_hTp, 1)

            def down(i, cur, e):
                for c in range(FC):
                    if c == FC // 2:
                        pe.wait_ge(s_hT, 2 * i + 2)
                    block, rows_c = bass.ds(e * FC + c, 1), slice(c * P, (c + 1) * P)
                    wide = (psO[:, 0:2 * D], hTh[:, cur, rows_c], w2[:, block].rearrange("p x l d -> p (x l d)"))
                    narrow = (psO[:, 0:D], hTl[:, cur, rows_c], w2[:, block, 0, :].rearrange("p x d -> p (x d)"))
                    for x in ((wide, narrow) if c == 0 else (narrow, wide)):
                        ins = pe.matmul(*x, start=(c == 0 and x is wide), stop=(c == FC - 1 and x is wide))
                ins.then_inc(s_y, 1)

            pe.wait_ge(s_route, 1)
            pe.wait_ge(s_wlo, len(CHUNKS))
            for c in range(2):
                drained(pe, ("rank", c))
            slot_T(0, 0, 0)
            up(0, 0, load_expert(0))
            slot_T(1, 1, 0)
            hidden_T(0, 0)
            up(1, 1, load_expert(1))
            with pe.Fori(0, SLOT_TILES // 2 - 1) as pair:
                for u in range(2):
                    i = 2 * pair + u
                    e, e2 = load_expert(i), load_expert(i + 2)
                    slot_T(i + 2, u, pair + 1, True)
                    down(i, u, e)
                    hidden_T(i + 1, 1 - u)
                    up(i + 2, u, e2)
            for i in range(SLOT_TILES - 2, SLOT_TILES):
                e = load_expert(i)
                pe.wait_ge(s_hT, 2 * i + 1)
                down(i, i % 2, e)
                if i == SLOT_TILES - 2:
                    hidden_T(i + 1, 1)

        @block.vector
        def _(dve):
            steps = [0]

            def link(ins):
                steps[0] += 1
                ins.then_inc(s_chain, 1)
                dve.wait_ge(s_chain, steps[0])

            def refine(n0, n1, k):
                v, r, t = ve[:, n0:n1], r0[:, n0:n1], rn[:, n0:n1]
                dve.wait_ge(s_r0, k)
                link(dve.tensor_tensor(t, r, r, ALU.mult))
                link(dve.tensor_tensor(t, t, v, ALU.mult))
                link(dve.tensor_scalar(t, t, -0.5, 1.5, ALU.mult, ALU.add))
                link(dve.tensor_tensor(rstd[:, n0:n1], t, r, ALU.mult))

            def normalise(i):
                n = rows_of(i % TT)
                return dve.tensor_scalar(xn[0:n, i, :], h_all[0:n, i, :], mv[0:n, i, 0:1], rstd[0:n, i:i + 1],
                                         ALU.subtract, ALU.mult)

            def moments(i):
                n = rows_of(i % TT)
                link(dve.bn_stats(stats[0:n, i, :], h_all[0:n, i, :]))
                dve.bn_aggr(mv[0:n, i, :], stats[0:n, i, :]).then_inc(s_chain, 1)
                steps[0] += 1

            def split(step, n, buf):
                high, middle, low = (qkp[0:n, buf, part, :] for part in range(3))
                if step == 0:
                    link(dve.tensor_copy(high, qk[0:n, buf, :]))
                    return dve.tensor_tensor(rest[0:n, :], qk[0:n, buf, :], high, ALU.subtract)
                link(dve.tensor_copy(middle, rest[0:n, :]))
                return dve.tensor_tensor(low, rest[0:n, :], middle, ALU.subtract)

            dve.wait_ge(ld_cst, 16)
            link(dve.tensor_copy(identb[:], ident))
            dve.wait_ge(s_const, N_CONST)

            def image(b):
                job_done(dve, ("img", b, 0))
                dve.tensor_tensor(h_all[0:NIMG, b * TT + TT - 1, :], bank(("img", b, 0))[0:NIMG, 0:D], pos[:],
                                  ALU.add).then_inc(s_dr["D"], 1)
                drained(dve, ("img", b, 0))

            def variances(n0, n1):
                dve.wait_ge(s_chain, steps[0])
                dve.tensor_scalar(ve[:, n0:n1], mv[:, n0:n1, 1], EPS, None, ALU.add).then_inc(s_var, 1)

            drained(dve, ("mem", 0))
            for step in range(2):
                link(split(step, MEM, 0))
            dve.sem_inc(s_memsplit, 1)
            dve.wait_ge(ld_first, 16)
            for t in range(TT - 1):
                moments(t)
            dve.wait_ge(ld_img, 64)
            image(0)
            moments(TT - 1)
            variances(0, TT)
            refine(0, TT, 1)
            dve.wait_ge(ld_txt, 16 * (B - 1))

            for s in ORDER:
                kind = s[0]
                if kind in ("gates", "wload", "whi", "swap"):
                    continue
                i = s[1]
                b, t = divmod(i, TT)
                n = rows_of(t)
                if kind == "img":
                    image(i)
                elif kind == "moments":
                    moments(i)
                elif kind == "first":
                    variances(TT, NT)
                    refine(TT, NT, 2)
                elif kind == "ln1":
                    normalise(i).then_inc(s_xn, 1)
                elif kind == "split":
                    if s[2] == 0:
                        drained(dve, ("qk", i, 0))
                        job_done(dve, ("stack", i - 2, 1, 0) if i >= 2 else ("memT", 1))
                    link(split(s[2], n, i % 2))
                    dve.sem_inc(s_split, 1)
                elif kind == "max":
                    _, g, t, j = s
                    n = rows_of(t)
                    job_done(dve, s + (0,))
                    if t == TT - 1:
                        rows2 = bank(s + (0,))[0:SIDE + n]
                        if j < 2:
                            ins = dve.tensor_reduce(mx[0:SIDE + n, g % 2, t, j:j + 1], rows2, AX, ALU.max)
                        else:
                            ins = dve.tensor_reduce(mt[0:SIDE + n, g % 2, t, 0:2],
                                                    rows2[:, 0:2 * P].rearrange("p (j l k) -> p j l k", j=2, l=2), AX, ALU.max)
                    elif j < GH:
                        ins = dve.tensor_reduce(mx[0:n, g % 2, t, j:j + 1], bank(s + (0,))[0:n, :], AX, ALU.max)
                    else:
                        ins = dve.tensor_reduce(mt[0:n, g % 2, t], bank(s + (0,))[0:n, :].rearrange("p (j l k) -> p j l k", j=GH, l=2), AX, ALU.max)
                    ins.then_inc(s_dr["D"], 1)
                elif kind == "negmax":
                    g = s[1]
                    u = g % 2
                    drained(dve, ("max", g, TT - 1, 2, 0))
                    if g >= 2:
                        dve.wait_ge(s_ring, PLACE[("maxT", g - 2, 0)] + 1)
                    link(dve.tensor_tensor(mt[:, u, :, :, 0], mx[:, u], mt[:, u, :, :, 0], ALU.max))
                    m = mt[:, u].rearrange("p t j l -> p (t j) l")
                    parts = mp[:, u].rearrange("p t j (l c) -> p (t j) l c", c=2)
                    link(dve.tensor_scalar(parts[:, :, :, 0], m, -1.0, None, ALU.mult))
                    dve.scalar_tensor_tensor(out=parts[:, :, :, 1], in0=m, scalar=-1.0, in1=parts[:, :, :, 0],
                                             op0=ALU.mult, op1=ALU.subtract).then_inc(s_neg, 1)
                elif kind == "norm":
                    u, l = i % 2, s[2]
                    job_done(dve, s + (0,))
                    src = bank(s + (0,))[0:n, 0:G * P].rearrange("p (g j w) -> p g j w", g=G, w=VW)
                    link(dve.reciprocal(rec[0:n, l], src[:, :, :, HD]))
                    r = rec[0:n, l].rearrange("p g (j o) -> p g j o", o=1).to_broadcast([n, G, GH, HD])
                    dve.tensor_tensor(prod[0:n, l], src[:, :, :, 0:HD], r, ALU.mult).then_inc(s_dr["D"], 1)
                    if l == 0:
                        continue
                    if i >= 2:
                        dve.wait_ge(s_ring, PLACE[("attT", i - 2, 0)] + 1)
                    drained(dve, s + (0,))
                    dve.tensor_tensor(att[0:n, u, :], prod[0:n, 0].rearrange("p g j d -> p (g j d)"),
                                      prod[0:n, 1].rearrange("p g j d -> p (g j d)"), ALU.add).then_inc(s_att, 1)
                    dve.wait_ge(s_att, i + 1)
                elif kind == "proj":
                    job_done(dve, s + (0,))
                    dve.tensor_tensor(h_all[0:n, i, :], bank(s + (0,))[0:n, 0:D], h_all[0:n, i, :], ALU.add).then_inc(s_dr["D"], 1)
                    drained(dve, s + (0,))
                    moments(i)
                elif kind == "rstd":
                    b = s[1]
                    variances(b * TT, (b + 1) * TT)
                    refine(b * TT, (b + 1) * TT, b + 3)
                elif kind == "ln2":
                    normalise(i).then_inc(s_ln2, 1)
                elif kind == "router":
                    job_done(dve, s + (0,))
                    dve.tensor_copy(logit[0:n, i, :], bank(s + (0,))[0:n, 0:NE]).then_inc(s_dr["D"], 1)

            drained(dve, ("router", NT - 1, 0))
            wide = lambda x: x.rearrange("p (i o) -> p i o", o=1).to_broadcast([P, NT, NE])
            pref = cst[:, C_PREF:C_PREF + NE].rearrange("p (o e) -> p o e", o=1).to_broadcast([P, NT, NE])
            work = logit
            for c in range(2):
                m = m12[:, c, :]
                link(dve.tensor_reduce(m, work[:], AX, ALU.max))
                link(dve.tensor_tensor(w8[:], work[:], wide(m), ALU.is_equal))
                link(dve.tensor_tensor(w8[:], w8[:], pref, ALU.mult))
                link(dve.tensor_reduce(dd[:], w8[:], AX, ALU.max))
                link(dve.tensor_tensor(oh[:, c], w8[:], wide(dd[:]), ALU.is_equal))
                if c == 0:
                    link(dve.tensor_scalar(w8b[:], oh[:, 0], -3.0e38, None, ALU.mult))
                    link(dve.tensor_tensor(posn[:], logit[:], w8b[:], ALU.add))
                    work = posn
            valid = cst[:, C_VALID:C_VALID + NT]
            for c in range(2):
                link(dve.tensor_tensor(oh[:, c], oh[:, c], wide(valid), ALU.mult))
            dve.tensor_tensor(both[:], oh[:, 0], oh[:, 1], ALU.add).then_inc(s_hot, 1)
            dve.tensor_tensor(w8[:], logit[:], wide(m12[:, 0, :]), ALU.subtract).then_inc(s_shift, 1)
            dve.tensor_tensor(dd[:], m12[:, 1, :], m12[:, 0, :], ALU.subtract).then_inc(s_shift, 1)
            job_done(dve, ("rank", 0))
            job_done(dve, ("rank", 1))
            rank = bank(("rank", 0))[:, 0:NT * NE].rearrange("p (i e) -> p i e", e=NE)
            total = bank(("rank", 1))[:, 0:NT * NE].rearrange("p (i e) -> p i e", e=NE)
            link(dve.memset(pre[:, :, 0:1, :], 0.0))
            link(dve.tensor_copy(pre[:, 0, 1:NT + 1, :], total))
            cur, step = 0, 1
            while step < NT:
                dve.tensor_copy(pre[:, 1 - cur, 1:1 + step, :], pre[:, cur, 1:1 + step, :]).then_inc(s_chain, 1)
                steps[0] += 1
                link(dve.tensor_tensor(pre[:, 1 - cur, 1 + step:NT + 1, :], pre[:, cur, 1 + step:NT + 1, :],
                                       pre[:, cur, 1:NT + 1 - step, :], ALU.add))
                cur, step = 1 - cur, 2 * step
            count = pre[:, cur, NT:NT + 1, :].rearrange("p o e -> p e o").to_broadcast([P, NE, EXP_TILES])
            kk = cst[:, C_K:C_K + EXP_TILES].rearrange("p (o k) -> p o k", o=1).to_broadcast([P, NE, EXP_TILES])
            link(dve.tensor_tensor(cmp[:], count, kk, ALU.is_gt))
            link(dve.tensor_reduce(nt_e[:], cmp[:], AX, ALU.add))
            link(dve.tensor_copy(end[:, 0, :], nt_e[:]))
            u, step = 0, 1
            while step < NE:
                dve.tensor_copy(end[:, 1 - u, 0:step], end[:, u, 0:step]).then_inc(s_chain, 1)
                steps[0] += 1
                link(dve.tensor_tensor(end[:, 1 - u, step:NE], end[:, u, step:NE], end[:, u, 0:NE - step], ALU.add))
                u, step = 1 - u, 2 * step
            link(dve.tensor_tensor(base[:], end[:, u, :], nt_e[:], ALU.subtract))
            link(dve.tensor_scalar(base[:], base[:], float(P), None, ALU.mult))
            link(dve.tensor_tensor(posn[:], rank, pre[:, cur, 0:NT, :], ALU.add))
            link(dve.tensor_tensor(posn[:], posn[:], base[:].rearrange("p (o e) -> p o e", o=1).to_broadcast([P, NT, NE]), ALU.add))
            for c in range(2):
                link(dve.tensor_tensor(both[:], oh[:, c], posn[:], ALU.mult))
                link(dve.tensor_reduce(slotf[:, c, :], both[:], AX, ALU.add))
            link(dve.tensor_copy(slot[:], slotf[:]))
            tau = cst[:, C_TAU:C_TAU + SLOT_TILES].rearrange("p (t o) -> p t o", o=1).to_broadcast([P, SLOT_TILES, NE])
            ends = end[:, u, :].rearrange("p (o e) -> p o e", o=1).to_broadcast([P, SLOT_TILES, NE])
            link(dve.tensor_tensor(tcmp[:], tau, ends, ALU.is_ge))
            link(dve.tensor_reduce(texf[:], tcmp[:], AX, ALU.add))
            link(dve.tensor_scalar(texf[:], texf[:], float(NE - 1), None, ALU.min))
            link(dve.tensor_copy(tex[:], texf[:]))
            dve.sem_inc(s_dr["D"], 2)
            link(dve.tensor_scalar(within_i[:], slot[:], P - 1, None, ALU.bitwise_and))
            link(dve.tensor_scalar(tile_i[:], slot[:], P.bit_length() - 1, None, ALU.logical_shift_right))
            link(dve.tensor_copy(within[:], within_i[:]))
            link(dve.tensor_copy(tile[:], tile_i[:]))
            dve.wait_ge(s_p, 2)
            link(dve.tensor_reduce(gsum[:], w8b[:], AX, ALU.add))
            link(dve.reciprocal(gw[:, 0, :], gsum[:]))
            link(dve.tensor_tensor(gw[:, 1, :], gw[:, 1, :], gw[:, 0, :], ALU.mult))
            for c in range(2):
                weight = weights[:, c].rearrange("p i w -> p w i")
                link(dve.tensor_tensor(gw[:, c, :], gw[:, c, :], valid, ALU.mult))
                dve.tensor_copy(weight[:, 0, :], cst[:, C_ROW:C_ROW + NT])
                link(dve.tensor_copy(weight[:, 1, :], gw[:, c, :]))
                link(dve.tensor_tensor(weight[:, 2, :], gw[:, c, :], weight[:, 1, :], ALU.subtract))
            dve.wait_ge(s_hst, 16 * (NT + 1))
            dve.wait_ge(s_xst, 16 * (2 * NT + 1))
            for q in range(2 * NT // HOTS):
                c, i = divmod(q * HOTS, NT)
                if q >= 2:
                    dve.wait_ge(s_list, q - 1)
                column = lambda x, n: x[:, c, i:i + HOTS].rearrange("p (j o) -> p j o", o=1).to_broadcast([P, HOTS, n])
                col = cst[:, C_COL:C_COL + P].rearrange("p (o s) -> p o s", o=1).to_broadcast([P, HOTS, P])
                dve.tensor_tensor(hot[:, q % 2], col, column(within, P), ALU.is_equal)
                taus = cst[:, C_TAU:C_TAU + SLOT_TILES].rearrange("p (o t) -> p o t", o=1).to_broadcast([P, HOTS, SLOT_TILES])
                link(dve.tensor_tensor(at[:], taus, column(tile, SLOT_TILES), ALU.is_equal))
                x = at[:].rearrange("p j (o t) -> p j o t", o=1).to_broadcast([P, HOTS, 3, SLOT_TILES])
                y = weights[:, c, i:i + HOTS].rearrange("p j (w o) -> p j w o", o=1).to_broadcast([P, HOTS, 3, SLOT_TILES])
                link(dve.tensor_tensor(sel[:, q % 2], x, y, ALU.mult))
                dve.sem_inc(s_onehot, 1)
            dve.wait_ge(s_list, 2 * NT // HOTS)
            link(dve.tensor_copy(gate_of[:], psO[:, 2 * SLOT_TILES:3 * SLOT_TILES]))
            link(dve.tensor_tensor(gate_of[:], psO[:, SLOT_TILES:2 * SLOT_TILES], gate_of[:], ALU.add))
            link(dve.tensor_scalar(row1[:], psO[:, 0:SLOT_TILES], 0.0, cst[:, C_EMPTY:C_EMPTY + 1], ALU.is_equal, ALU.mult))
            link(dve.scalar_tensor_tensor(out=rowf[:], in0=psO[:, 0:SLOT_TILES], scalar=-1.0, in1=row1[:], op0=ALU.add, op1=ALU.add))
            link(dve.tensor_copy(row[:], rowf[:]))
            dve.sem_inc(s_route, 1)

            def slot_T(i, cur):
                dve.wait_ge(s_mx, i + 1)
                dve.wait_ge(s_h, i - 1) if not isinstance(i, int) or i >= 2 else None
                dve.tensor_copy(xh[:, cur, :], ring[0][:, 0:2 * P]).then_inc(s_xh, 1)
                dve.wait_ge(s_xh, i + 1)
                dve.tensor_tensor(xl[:, cur, :], ring[0][:, 0:2 * P], xh[:, cur, :], ALU.subtract).then_inc(s_mxT, 1)

            def low(i, cur):
                for half in range(2):
                    cols = slice(half * W, (half + 1) * W)
                    dve.wait_ge(s_hThi, 2 * i + 1 + half)
                    dve.tensor_tensor(hTl[:, cur, cols], ring[1 + half][:, 0:W], hTh[:, cur, cols],
                                      ALU.subtract).then_inc(s_hT, 1)

            def total(i, cur):
                dve.wait_ge(s_y, i + 1)
                dve.wait_ge(s_ysb, i - 1) if not isinstance(i, int) or i >= 2 else None
                dve.tensor_copy(ysum[:, cur, :], psO[:, D:2 * D]).then_inc(s_half, 1)
                dve.wait_ge(s_half, i + 1)
                dve.tensor_tensor(ysum[:, cur, :], psO[:, 0:D], ysum[:, cur, :], ALU.add).then_inc(s_ysum, 1)

            slot_T(0, 0)
            slot_T(1, 1)
            for i in range(2):
                low(i, i)
                slot_T(i + 2, i)
                total(i, i)
            with dve.Fori(1, SLOT_TILES // 2 - 1) as pair:
                for u in range(2):
                    i = 2 * pair + u
                    low(i, u)
                    slot_T(i + 2, u)
                    total(i, u)
            for i in range(SLOT_TILES - 2, SLOT_TILES):
                low(i, i % 2)
                total(i, i % 2)


def kernel(x, txt, L0_tok_W, L0_tok_b, L0_tok_class_token, L0_tok_pos_embedding, L0_attn_w_qkv, L0_attn_b_qkv,
           L0_attn_w_out, L0_attn_b_out, L0_attn_w_mem, L0_attn_b_mem, L0_attn_memory, L0_ffn_router_w,
           L0_ffn_w1, L0_ffn_w2):
    import numpy as np
    import concourse.bacc as bacc
    from concourse.bass_utils import run_bass_kernel_spmd

    f = lambda v: np.asarray(v)
    s = 16
    n = 96 // s
    x = f(x)
    pt = x.reshape(B, 3, n, s, n, s).transpose(0, 1, 2, 4, 3, 5).reshape(B, NPATCH, PD).transpose(2, 0, 1)
    patchT = np.zeros((PC, P, B, NIMG), x.dtype)
    patchT[:, :, :, 1:] = pt.reshape(PC, P, B, NPATCH)
    with_row = lambda w, row: np.concatenate([w, row.reshape(1, -1)], 0)
    cst = np.zeros((P, C_N), np.float32)
    cst[:, C_ID:C_ID + P] = np.eye(P)
    cst[:, C_TRI:C_TRI + P] = np.triu(np.ones((P, P)), 1)
    cst[:, C_ONE:C_ONE + P] = 1
    cst[:, C_PREF:C_PREF + NE] = NE - np.arange(NE)
    cst[:, C_TAU:C_TAU + SLOT_TILES] = np.arange(SLOT_TILES)
    cst[:, C_K:C_K + EXP_TILES] = P * np.arange(EXP_TILES)
    for i in range(NT):
        cst[0:rows_of(i % TT), C_VALID + i] = 1
    cst[0, C_SEL] = 1
    cst[1, C_SEL + 1:C_SEL + NIMG] = 1
    for i in range(NT):
        b, t = divmod(i, TT)
        r = np.arange(rows_of(t))
        cst[r, C_ROW + i] = b * T + (NIMG + t * P if t < TT - 1 else 0) + r + 1
    cst[:, C_EMPTY] = B * T + np.arange(P) + 1
    cst[:, C_COL:C_COL + P] = np.arange(P)
    koff = np.zeros((KM - KQ, KEYS), np.float32)
    koff[0:2, 0:KEYS - MEM] = 1
    koff[2:4, KEYS - MEM:KEYS] = 1
    mem = f(L0_attn_memory)[0]
    arrays = {
        "cst": cst,
        "patchT": patchT.transpose(1, 0, 2, 3),
        "tokw": f(L0_tok_W).T.reshape(PC, P, D).transpose(1, 0, 2),
        "clsb": np.concatenate([f(L0_tok_class_token), f(L0_tok_b).reshape(1, -1)], 0),
        "pos": f(L0_tok_pos_embedding),
        "txt": f(txt),
        "wqkv": with_row(f(L0_attn_w_qkv), f(L0_attn_b_qkv)),
        "wout": with_row(f(L0_attn_w_out), f(L0_attn_b_out)),
        "wmem": with_row(f(L0_attn_w_mem), f(L0_attn_b_mem)),
        "koff": koff,
        "memT": with_row(mem.T, np.ones(MEM, mem.dtype)),
        "wr": f(L0_ffn_router_w).T,
        "w1": f(L0_ffn_w1).transpose(1, 0, 2).reshape(D, NE * DFF),
        "w2": f(L0_ffn_w2).reshape(NE, FC, P, D).transpose(2, 0, 1, 3).reshape(P, NE * FC * D),
    }
    nc = bacc.Bacc("TRN2", target_bir_lowering=False, num_devices=1)
    ins, aps = {}, {}
    for name, v in arrays.items():
        v = np.ascontiguousarray(v)
        ins["in_" + name] = v
        aps[name] = nc.dram_tensor("in_" + name, v.shape, mybir.dt.from_np(v.dtype), kind="ExternalInput").ap()
    out = nc.dram_tensor("out", (NROWS, D), F32, kind="ExternalOutput").ap()
    build(nc, aps, out)
    r = run_bass_kernel_spmd(nc, [ins], core_ids=[0])
    return r.results[0]["out"][0:B * T].reshape(B, T, D)
```
